# Optimizing a Trainium2 kernel written in Bass

```python
import numpy as np
import jax
import jax.numpy as jnp

def _softmax(x, axis=-1):
    return jax.nn.softmax(x, axis=axis)

def _gelu(x):
    return jax.nn.gelu(x, approximate=True)

def _silu(x):
    return jax.nn.silu(x)

def _sigmoid(x):
    return jax.nn.sigmoid(x)

def _layernorm(x, axis=-1, eps=1e-05):
    m = jnp.mean(x, axis=axis, keepdims=True)
    v = jnp.var(x, axis=axis, keepdims=True)
    return (x - m) / jnp.sqrt(v + eps)

def _scatter_add(tgt, idx, src, axis=0):
    return tgt.at[idx].add(src)

def _segment_sum(src, seg, n):
    return jax.ops.segment_sum(src, seg, n)
kernel_name = 'mk_gnn_resnorm_d1_gnn_r8_10d2af'

def setup_inputs(seed: int=0):
    np.random.seed(seed)
    _w = jnp.asarray

    def _rec_inputs():
        import jax
        import jax.numpy as jnp
        _gk = jax.random.key(seed)
        x = -0.0003713 + 1 * jax.random.normal(jax.random.fold_in(_gk, 1), (6250, 256), jnp.float32)
        _s = jax.random.randint(jax.random.fold_in(_gk, 2), (100000,), 0, 6250, jnp.int32)
        _d = jax.random.randint(jax.random.fold_in(_gk, 3), (100000,), 0, 6250, jnp.int32)
        _loop = jnp.arange(6250, dtype=jnp.int32)
        src = jnp.concatenate([_s, _d, _loop])
        dst = jnp.concatenate([_d, _s, _loop])
        _o = jnp.argsort(dst, stable=True)
        src = src[_o]
        dst = dst[_o]
        edge_attr_16 = -0.000153872 + 1.00011 * jax.random.normal(jax.random.fold_in(_gk, 11), (206250, 16), jnp.float32)
        edge_attr_4 = 0.0007022 + 0.999661 * jax.random.normal(jax.random.fold_in(_gk, 12), (206250, 4), jnp.float32)
        return (x, src, dst, edge_attr_16, edge_attr_4)
    x, src, dst, edge_attr_16, edge_attr_4 = _rec_inputs()

    def _L0_gnn_setup():
        import jax, jax.numpy as jnp
        import numpy as np
        N, E, C, R, HID = (6250, 62500, 64, 16, 64)
        key = jax.random.key(seed)
        ks = jax.random.split(key, 24)
        g = lambda k, shape, s=1.0: jax.random.normal(k, shape, dtype=jnp.float32) * s
        cs = C ** (-0.5)
        inp = {'h': g(ks[0], (N, 4 * C)), 'edge_index': jax.random.randint(ks[1], (2, E), 0, N), 'edge_sh': g(ks[2], (E, 4)), 'edge_rbf': g(ks[3], (E, R)), 'W_up0': g(ks[4], (C, C), cs), 'W_up1': g(ks[5], (C, C), cs), 'M1': g(ks[6], (R, HID), R ** (-0.5)), 'M2': g(ks[7], (HID, HID), HID ** (-0.5)), 'M3': g(ks[8], (HID, HID), HID ** (-0.5)), 'M4': g(ks[9], (HID, 4 * C), HID ** (-0.5)), 'W_lin0': g(ks[10], (C, C), cs), 'W_lin1': g(ks[11], (C, C), cs), 'Wsc0': g(ks[12], (C, C), cs), 'Wsc1': g(ks[13], (C, C), cs), 'Wc0': g(ks[14], (C, 5)), 'Wc1': g(ks[15], (C, 4)), 'WB0': g(ks[16], (C, C), cs), 'WB1': g(ks[17], (C, C), cs), 'gamma0': jnp.ones((C,), jnp.float32), 'beta0': jnp.zeros((C,), jnp.float32), 'gamma1': jnp.ones((C,), jnp.float32)}
        return inp
    _L0_gnn_all = _L0_gnn_setup()
    _L0_gnn_in = {k: v for k, v in _L0_gnn_all.items() if k in ('W_up0', 'W_up1', 'M1', 'M2', 'M3', 'M4', 'W_lin0', 'W_lin1', 'Wsc0', 'Wsc1', 'Wc0', 'Wc1', 'WB0', 'WB1', 'gamma0', 'beta0', 'gamma1')}
    del _L0_gnn_all
    return {'x': x, 'src': src, 'dst': dst, 'edge_attr_16': edge_attr_16, 'edge_attr_4': edge_attr_4, 'L0_gnn_W_up0': _L0_gnn_in['W_up0'], 'L0_gnn_W_up1': _L0_gnn_in['W_up1'], 'L0_gnn_M1': _L0_gnn_in['M1'], 'L0_gnn_M2': _L0_gnn_in['M2'], 'L0_gnn_M3': _L0_gnn_in['M3'], 'L0_gnn_M4': _L0_gnn_in['M4'], 'L0_gnn_W_lin0': _L0_gnn_in['W_lin0'], 'L0_gnn_W_lin1': _L0_gnn_in['W_lin1'], 'L0_gnn_Wsc0': _L0_gnn_in['Wsc0'], 'L0_gnn_Wsc1': _L0_gnn_in['Wsc1'], 'L0_gnn_Wc0': _L0_gnn_in['Wc0'], 'L0_gnn_Wc1': _L0_gnn_in['Wc1'], 'L0_gnn_WB0': _L0_gnn_in['WB0'], 'L0_gnn_WB1': _L0_gnn_in['WB1'], 'L0_gnn_gamma0': _L0_gnn_in['gamma0'], 'L0_gnn_beta0': _L0_gnn_in['beta0'], 'L0_gnn_gamma1': _L0_gnn_in['gamma1']}

def reference(x, src, dst, edge_attr_16, edge_attr_4, L0_gnn_W_up0, L0_gnn_W_up1, L0_gnn_M1, L0_gnn_M2, L0_gnn_M3, L0_gnn_M4, L0_gnn_W_lin0, L0_gnn_W_lin1, L0_gnn_Wsc0, L0_gnn_Wsc1, L0_gnn_Wc0, L0_gnn_Wc1, L0_gnn_WB0, L0_gnn_WB1, L0_gnn_gamma0, L0_gnn_beta0, L0_gnn_gamma1):
    import jax
    import jax.numpy as jnp

    def _L0_gnn_ref(h, edge_index, edge_sh, edge_rbf, W_up0, W_up1, M1, M2, M3, M4, W_lin0, W_lin1, Wsc0, Wsc1, Wc0, Wc1, WB0, WB1, gamma0, beta0, gamma1):
        import jax, jax.numpy as jnp
        import numpy as np
        N, E, C, R, HID = (6250, 62500, 64, 16, 64)
        n = h.shape[0]
        h0 = h[:, :C]
        h1 = h[:, C:].reshape(n, C, 3)
        up0 = h0 @ W_up0
        up1 = jnp.einsum('ncx,cd->ndx', h1, W_up1)
        r = jax.nn.silu(edge_rbf @ M1)
        r = jax.nn.silu(r @ M2)
        r = jax.nn.silu(r @ M3)
        tpw = (r @ M4).reshape(-1, 4, C)
        snd, rcv = (edge_index[0], edge_index[1])
        x0 = up0[snd]
        x1 = up1[snd]
        sh0 = edge_sh[:, 0]
        sh1 = edge_sh[:, 1:]
        inv3 = 1.0 / jnp.sqrt(jnp.float32(3.0))
        m0e = tpw[:, 0] * x0 * sh0[:, None] + tpw[:, 3] * jnp.einsum('ecx,ex->ec', x1, sh1) * inv3
        m1e = tpw[:, 1][:, :, None] * x0[:, :, None] * sh1[:, None, :] + tpw[:, 2][:, :, None] * x1 * sh0[:, None, None]
        msg0 = jax.ops.segment_sum(m0e, rcv, num_segments=n)
        msg1 = jax.ops.segment_sum(m1e, rcv, num_segments=n)
        A0 = msg0 @ W_lin0
        A1 = jnp.einsum('ncx,cd->ndx', msg1, W_lin1)
        sc0 = h0 @ Wsc0
        sc1 = jnp.einsum('ncx,cd->ndx', h1, Wsc1)
        vv = jnp.sum(A1 * A1, -1)
        B0 = Wc0[:, 0] * A0 + Wc0[:, 1] * A0 * A0 + Wc0[:, 2] * vv + Wc0[:, 3] * A0 ** 3 + Wc0[:, 4] * A0 * vv
        B1 = (Wc1[:, 0] + Wc1[:, 1] * A0 + Wc1[:, 2] * A0 * A0 + Wc1[:, 3] * vv)[..., None] * A1
        o0 = B0 @ WB0 + sc0
        o1 = jnp.einsum('ncx,cd->ndx', B1, WB1) + sc1
        eps = jnp.float32(1e-05)
        mu = jnp.mean(o0, 0)
        xc = o0 - mu
        var = jnp.mean(xc * xc, 0)
        n0 = xc * jax.lax.rsqrt(var + eps) * gamma0 + beta0
        nrm1 = jnp.mean(jnp.sum(o1 * o1, -1) / 3.0, 0)
        n1 = o1 * (jax.lax.rsqrt(nrm1 + eps) * gamma1)[None, :, None]
        return jnp.concatenate([n0, n1.reshape(n, 3 * C)], -1)
    edge_index = jnp.stack([src, dst])
    x = _layernorm(x + _L0_gnn_ref(x, edge_index, edge_attr_4, edge_attr_16, L0_gnn_W_up0, L0_gnn_W_up1, L0_gnn_M1, L0_gnn_M2, L0_gnn_M3, L0_gnn_M4, L0_gnn_W_lin0, L0_gnn_W_lin1, L0_gnn_Wsc0, L0_gnn_Wsc1, L0_gnn_Wc0, L0_gnn_Wc1, L0_gnn_WB0, L0_gnn_WB1, L0_gnn_gamma0, L0_gnn_beta0, L0_gnn_gamma1), axis=-1)
    return x

_drawn_inputs = setup_inputs


def setup_inputs(seed=0):
    import zlib

    import numpy as np

    out = dict(_drawn_inputs(seed))
    spreads = {'L0_gnn_gamma0': (1.0, 0.2), 'L0_gnn_beta0': (0.0, 0.1), 'L0_gnn_gamma1': (1.0, 0.2)}
    factors = {'L0_gnn_Wsc0': 3.198}
    for name, (base, spread) in spreads.items():
        noise = np.random.default_rng([zlib.crc32(name.encode()), seed]).standard_normal(out[name].shape)
        drawn = base * np.exp(spread * noise) if base else spread * noise
        out[name] = jnp.asarray(drawn.astype(out[name].dtype))
    for name, factor in factors.items():
        out[name] = (out[name] * factor).astype(out[name].dtype)
    return out
```

```python
from contextlib import ExitStack

import concourse.bass as bass
from concourse import mybir

P = 128
C = 64
COMP = 4
F = COMP * C
R = 16
N = 6250
E = 206250
G = 6
W = 32
SETCOLS = G // 2 * P
GROUPS = -(-E // (2 * G * P)) * 2
TILES = GROUPS * G
HALF = -(-N // (2 * P)) * P
NODES = 2 * HALF
CH = 320
CHUNKS = HALF // CH
UPT = 5
UPCHUNKS = NODES // (UPT * P)
NTILES = HALF // P
ACCW = NODES + W
EPS = 1e-5
TBLOCK = 90
assert HALF % CH == 0 and CHUNKS % 2 == 0 and UPCHUNKS % 2 == 0 and GROUPS % TBLOCK == 0
LAST_FULL = (N - HALF) // P
LAST_ROWS = N - HALF - LAST_FULL * P

(UP_A, UP_B, M2D, M3D, LIN0_A, LIN0_B, LIN1_A, LIN1_B, WB0D, WB1D, SC0D, SC1D) = range(12)

f32 = mybir.dt.float32
i32 = mybir.dt.int32
u32 = mybir.dt.uint32
ALU = mybir.AluOpType
ACT = mybir.ActivationFunctionType
X = mybir.AxisListType.X


def first(step, count=1):
    return isinstance(step, int) and step < count


def build(nc, x_pairs, x_sets, src, dst, sh, rbf, w, out):
    up_table = nc.dram_tensor("up_table", (NODES, F), f32, kind="Internal").ap()

    with ExitStack() as whole:
        def sb(name, shape, dt=f32, ctx=whole):
            return ctx.enter_context(nc.sbuf_tensor(name, shape, dt))

        def sem(name):
            return whole.enter_context(nc.semaphore(name))

        wts = sb("wts", [P, 12, P])
        m1d = sb("m1d", [2 * R, P])
        m4 = sb("m4", [P, 2, F])
        wc0 = sb("wc0", [P, 5])
        wc1 = sb("wc1", [P, 4])
        gamma0 = sb("gamma0", [P, 1])
        beta0 = sb("beta0", [P, 1])
        gamma1 = sb("gamma1", [P, 1])
        ident = sb("ident", [P, P])
        pair = sb("pair", [P, P])
        eps = sb("eps", [P, 1])
        acc = sb("acc", [P, 3, ACCW])

        load_weights(nc, w, wts, m1d, m4, wc0, wc1, gamma0, beta0, gamma1, ident, pair, eps, acc, sem)
        project_nodes(nc, x_pairs, wts, up_table, sem)
        with ExitStack() as edges:
            edge_phase(nc, edges, src, dst, sh, rbf, up_table, m1d, m4, wts, ident, acc, sem)
        with ExitStack() as nodes:
            node_phase(nc, nodes, x_sets, wts, wc0, wc1, gamma0, beta0, gamma1, ident, pair, eps, acc, out, sem)


def load_weights(nc, w, wts, m1d, m4, wc0, wc1, gamma0, beta0, gamma1, ident, pair, eps, acc, sem):
    cleared = sem("weights_cleared")
    pool_cleared = sem("constants_cleared")
    made = sem("constants_made")
    loaded = sem("weights_loaded")
    lo, hi = slice(0, C), slice(C, 2 * C)
    with nc.Block() as block:
        @block.vector
        def _(dve):
            nc.vector.memset(wts[:, :, :], 0.0).then_inc(cleared, 1)
            nc.vector.memset(m1d[:, :], 0.0).then_inc(cleared, 1)
            nc.vector.memset(m4[:, :, :], 0.0).then_inc(cleared, 1)
            nc.vector.memset(eps[:, :], EPS)
            nc.vector.memset(acc[:, :, :], 0.0)
            dve.wait_ge(loaded, 16 * 34)
            nc.vector.tensor_scalar(m4[:, :, 3 * C:4 * C], m4[:, :, 3 * C:4 * C], 3.0 ** -0.5, None, ALU.mult)

        @block.gpsimd
        def _(pool):
            nc.gpsimd.memset(ident[:, :], 0.0).then_inc(pool_cleared, 1)
            nc.gpsimd.memset(pair[:, :], 0.0).then_inc(pool_cleared, 1)
            pool.wait_ge(pool_cleared, 2)
            nc.gpsimd.affine_select(out=ident[:, :], in_=ident[:, :], compare_op=ALU.not_equal, fill=1.0,
                                    base=0, pattern=[[-1, P]], channel_multiplier=1).then_inc(made, 1)
            for n, shift in enumerate((0, C, -C)):
                nc.gpsimd.affine_select(out=pair[:, :], in_=pair[:, :], compare_op=ALU.not_equal, fill=1.0,
                                        base=shift, pattern=[[-1, P]], channel_multiplier=1).then_inc(made, 1)
                pool.wait_ge(made, n + 2)

        def put(eng, dst, src):
            eng.dma_start(dst, src).then_inc(loaded, 16)

        @block.sync
        def _(sp):
            sp.wait_ge(cleared, 3)
            for tile, a, b in ((UP_A, "W_up0", "W_up1"), (UP_B, "W_up1", "W_up1"), (M2D, "M2", "M2"),
                               (M3D, "M3", "M3"), (WB0D, "WB0", "WB0"), (WB1D, "WB1", "WB1"),
                               (SC0D, "Wsc0", "Wsc0"), (SC1D, "Wsc1", "Wsc1")):
                put(sp, wts[lo, tile, lo], w[a])
                put(sp, wts[hi, tile, hi], w[b])
            put(sp, m1d[0:R, lo], w["M1"])
            put(sp, m1d[R:2 * R, hi], w["M1"])

        @block.scalar
        def _(act):
            act.wait_ge(cleared, 3)
            put(act, wts[hi, LIN0_A, lo], w["W_lin0"])
            put(act, wts[hi, LIN0_B, hi], w["W_lin0"])
            put(act, wts[lo, LIN1_A, lo], w["W_lin1"])
            put(act, wts[lo, LIN1_B, hi], w["W_lin1"])
            put(act, m4[lo, 0, :], w["M4"])
            put(act, m4[hi, 1, :], w["M4"])
            for half in (lo, hi):
                put(act, wc0[half, :], w["Wc0"])
                put(act, wc1[half, :], w["Wc1"])
            for half in (lo, hi):
                put(act, gamma0[half, :], w["gamma0"].rearrange("(c a) -> c a", a=1))
                put(act, beta0[half, :], w["beta0"].rearrange("(c a) -> c a", a=1))
            put(act, gamma1[lo, :], w["gamma1"].rearrange("(c a) -> c a", a=1))

            put(act, gamma1[hi, :], w["gamma1"].rearrange("(c a) -> c a", a=1))


def project_nodes(nc, x_pairs, wts, up_table, sem):
    loaded = [sem(f"x_loaded{b}") for b in range(2)]
    stored = [sem(f"up_stored{b}") for b in range(2)]
    product = sem("up_product")
    moved = sem("up_moved")
    with ExitStack() as ctx:
        xin = ctx.enter_context(nc.sbuf_tensor("xin", [P, 2, 2, UPT * P], f32))
        up_out = ctx.enter_context(nc.sbuf_tensor("up_out", [P, 2, UPT, F], f32))
        up_ps = ctx.enter_context(nc.psum_tensor("up_ps", [P, 2, UPT + 1, F], f32))
        rows = up_table.rearrange("(n p) f -> p n f", p=P)
        block = ctx.enter_context(nc.Block())

        @block.sync
        def _(sp):
            def load(i, b):
                if not first(i):
                    sp.wait_ge(product, i * 2 + b - 1)
                sp.dma_start(xin[:, b, :, :], x_pairs[:, :, bass.ds((i * 2 + b) * (UPT * P), UPT * P)])\
                  .then_inc(loaded[b], 16)

            for b in range(2):
                load(0, b)
            with sp.Fori(1, UPCHUNKS // 2) as i:
                for b in range(2):
                    load(i, b)

        @block.tensor
        def _(pe):
            def multiply(i, b):
                pe.wait_ge(loaded[b], i * 16 + 16)
                if not first(i):
                    pe.wait_ge(moved, i * 2 + b - 1)
                for t in range(UPT):
                    nc.tensor.matmul(up_ps[:, b, t, 0:P], xin[:, b, 0, t * P:(t + 1) * P],
                                     wts[:, UP_A, :], start=True, stop=True)
                    last = nc.tensor.matmul(up_ps[:, b, t, P:2 * P], xin[:, b, 1, t * P:(t + 1) * P],
                                            wts[:, UP_B, :], start=True, stop=True)
                last.then_inc(product, 1)

            for b in range(2):
                multiply(0, b)
            with pe.Fori(1, UPCHUNKS // 2) as i:
                for b in range(2):
                    multiply(i, b)

        @block.vector
        def _(dve):
            def step(i):
                for b in range(2):
                    if not first(i):
                        dve.wait_ge(stored[b], i * 16)
                    dve.wait_ge(product, i * 2 + b + 1)
                    nc.vector.tensor_copy(up_out[:, b, :, :], up_ps[:, b, 0:UPT, :]).then_inc(moved, 1)

            step(0)
            with dve.Fori(1, UPCHUNKS // 2) as i:
                step(i)

        @block.scalar
        def _(act):
            def step(i):
                for b in range(2):
                    act.wait_ge(moved, i * 2 + b + 1)
                    act.dma_start(rows[:, bass.ds((i * 2 + b) * UPT, UPT), :], up_out[:, b, :, :])\
                       .then_inc(stored[b], 16)

            step(0)
            with act.Fori(1, UPCHUNKS // 2) as i:
                step(i)
            for b in range(2):
                act.wait_ge(stored[b], 16 * (UPCHUNKS // 2))


def edge_phase(nc, ctx, src, dst, sh, rbf, up_table, m1d, m4, wts, ident, acc, sem):
    def sb(name, shape, dt=f32):
        return ctx.enter_context(nc.sbuf_tensor(name, shape, dt))

    src_all = sb("src_all", [P, TILES], u32)
    rel = sb("rel", [P, TILES])
    sh_all = sb("sh_all", [P, TILES, COMP])
    start_row = sb("start_row", [1, GROUPS], i32)
    passes = sb("passes", [1, 1], i32)
    columns = sb("columns", [P, W])

    window_prelude(nc, src, dst, sh, src_all, rel, sh_all, start_row, passes, columns, ident, sem)

    idx = sb("idx", [P, 2, G], u32)
    rbf_t = sb("rbf_t", [2 * R, 2, SETCOLS])
    hid = sb("hid", [P, 2, SETCOLS])
    hid3 = sb("hid3", [P, 2, SETCOLS])
    xg = sb("xg", [P, 2, G, F])
    prod = sb("prod", [P, 2, G, 4, 2, C])
    onehot = sb("onehot", [P, G, W])
    shot = sb("shot", [P, 2, G, COMP, W])
    mlp_ps = ctx.enter_context(nc.psum_tensor("mlp_ps", [P, 512], f32))
    radial_ps = ctx.enter_context(nc.psum_tensor("radial_ps", [P, 2, G, F], f32))
    sum_ps = ctx.enter_context(nc.psum_tensor("sum_ps", [P, 4, P], f32))

    rbf_loaded = [sem(f"rbf_loaded{b}") for b in range(2)]
    gathered = [sem(f"gathered{b}") for b in range(2)]
    idx_staged = sem("idx_staged")
    gather_gate = sem("gather_gate")
    mlp_product = sem("mlp_product")
    mlp_active = sem("mlp_active")
    radial_ready = sem("radial_ready")
    onehot_made = sem("onehot_made")
    prod_ready = sem("prod_ready")
    summed = sem("summed")
    added = sem("added")
    scalar_added = sem("scalar_added")
    per_pass = [*rbf_loaded, *gathered, idx_staged, gather_gate, mlp_product, mlp_active,
                radial_ready, onehot_made, prod_ready, summed, added, scalar_added]

    n_passes = nc.values_load(passes[0:1, 0:1], min_val=1, max_val=N // W + 1)
    with nc.Fori(0, n_passes):
        with nc.Block() as block:
            @block.sync
            def _(sp):
                def load(i, b):
                    sp.dma_start(rbf_t[:, b, :], rbf[bass.ds(i * 2 + b, 1), :, :].rearrange("a r c -> r (a c)"))\
                      .then_inc(rbf_loaded[b], 16)

                for b in range(2):
                    load(0, b)
                with sp.Fori(1, GROUPS // 2) as i:
                    for b in range(2):
                        sp.wait_ge(mlp_product, (i * 2 + b - 2) * 3 + 1)
                        load(i, b)

            @block.scalar
            def _(act):
                def stage(i, b):
                    nc.scalar.copy(idx[:, b, :], src_all[:, bass.ds((i * 2 + b) * G, G)]).then_inc(idx_staged, 1)

                def layers(i, b):
                    for layer, dest in enumerate((hid[:, 0, :], hid[:, 1, :], hid3[:, b, :])):
                        act.wait_ge(mlp_product, (i * 2 + b) * 3 + layer + 1)
                        nc.scalar.activation(dest, mlp_ps[:, 0:SETCOLS], ACT.Silu).then_inc(mlp_active, 1)

                for b in range(2):
                    stage(0, b)
                layers(0, 0)
                with act.Fori(0, GROUPS // 2 - 1) as i:
                    for b in range(2):
                        layers(*((i, 1) if b == 0 else (i + 1, 0)))
                        act.wait_ge(gathered[b], (i + 1) * (16 * G))
                        stage(i + 1, b)
                layers(GROUPS // 2 - 1, 1)

            @block.gpsimd
            def _(pool):
                def gather(b):
                    for t in range(G):
                        nc.gpsimd.indirect_dma_start(
                            out=xg[:, b, t, :], out_offset=None, in_=up_table[:, :],
                            in_offset=bass.IndirectOffsetOnAxis(ap=idx[:, b, t:t + 1], axis=0))\
                          .then_inc(gathered[b], 16)

                for b in range(2):
                    pool.wait_ge(idx_staged, b + 1)
                    gather(b)
                with pool.Fori(1, GROUPS // 2) as i:
                    for b in range(2):
                        pool.wait_ge(prod_ready, i * 2 + b - 1)
                        pool.wait_ge(idx_staged, i * 2 + b + 1)
                        pool.sem_inc(gather_gate, 1)
                        gather(b)

            @block.vector
            def _(dve):
                def onehots(i, b):
                    g = i * 2 + b
                    tiles = bass.ds(g * G, G)
                    if not first(g):
                        dve.wait_ge(onehot_made, g * 2)
                    nc.vector.tensor_tensor(
                        onehot[:, :, :], columns[:, :].unsqueeze(1).broadcast_to([P, G, W]),
                        rel[:, tiles].unsqueeze(2).broadcast_to([P, G, W]), ALU.is_equal).then_inc(onehot_made, 1)
                    dve.wait_ge(onehot_made, g * 2 + 1)
                    nc.vector.tensor_tensor(
                        shot[:, b, :, :, :], onehot[:, :, :].unsqueeze(2).broadcast_to([P, G, COMP, W]),
                        sh_all[:, tiles, :].unsqueeze(3).broadcast_to([P, G, COMP, W]), ALU.mult)\
                      .then_inc(onehot_made, 1)

                def products(i, b):
                    dve.wait_ge(radial_ready, i * 2 + b + 1)
                    dve.wait_ge(gathered[b], (i + 1) * (16 * G))
                    rad, rows, o = radial_ps[:, b], xg[:, b], prod[:, b]
                    flat = o.rearrange("p t s h c -> p t (s h c)")
                    nc.vector.tensor_tensor(
                        o[:, :, 0:3, 0, :], rad[:, :, 2 * C:3 * C].unsqueeze(2).broadcast_to([P, G, 3, C]),
                        rows[:, :, C:4 * C].rearrange("p t (s c) -> p t s c", c=C), ALU.mult)
                    nc.vector.tensor_tensor(
                        o[:, :, 1:3, 1, :], rad[:, :, 3 * C:4 * C].unsqueeze(2).broadcast_to([P, G, 2, C]),
                        rows[:, :, 2 * C:4 * C].rearrange("p t (s c) -> p t s c", c=C), ALU.mult)
                    nc.vector.tensor_tensor(o[:, :, 3, 1, :], rad[:, :, 3 * C:4 * C], rows[:, :, C:2 * C], ALU.mult)
                    nc.vector.tensor_tensor(o[:, :, 0, 1, :], rad[:, :, 0:C], rows[:, :, 0:C], ALU.mult)
                    nc.vector.tensor_tensor(o[:, :, 3, 0, :], rad[:, :, C:2 * C], rows[:, :, 0:C], ALU.mult)\
                      .then_inc(prod_ready, 1)

                def add(i, b):
                    g = i * 2 + b
                    start = dve.value_load(start_row[0:1, bass.ds(g, 1)], min_val=0, max_val=N)
                    dve.wait_ge(summed, g + 1)
                    if not first(g):
                        dve.wait_ge(added, g)
                    vec = acc[0:C, :, bass.ds(start, W)]
                    nc.vector.tensor_tensor(vec, sum_ps[0:C, 0:3, 0:W], vec, ALU.add)
                    sca = acc[C:2 * C, 0, bass.ds(start, W)]
                    nc.vector.tensor_tensor(sca, sum_ps[C:2 * C, 0, 0:W], sca, ALU.add).then_inc(scalar_added, 1)
                    dve.wait_ge(scalar_added, g + 1)
                    nc.vector.tensor_tensor(sca, sum_ps[C:2 * C, 3, 0:W], sca, ALU.add).then_inc(added, 1)

                onehots(0, 0)
                products(0, 0)
                onehots(0, 1)
                add(0, 0)
                products(0, 1)
                with dve.Fori(1, GROUPS // 2) as i:
                    for b in range(2):
                        dve.wait_ge(summed, i * 2 + b - 1)
                        onehots(i, b)
                        add(*((i - 1, 1) if b == 0 else (i, 0)))
                        products(i, b)
                add(GROUPS // 2 - 1, 1)

            @block.tensor
            def _(pe):
                def layer(i, b, n):
                    g = i * 2 + b
                    if n == 0:
                        pe.wait_ge(rbf_loaded[b], i * 16 + 16)
                    if n or not first(g):
                        pe.wait_ge(mlp_active, g * 3 + n)
                    weight = (m1d[:, :], wts[:, M2D, :], wts[:, M3D, :])[n]
                    data = (rbf_t[:, b, :], hid[:, 0, :], hid[:, 1, :])[n]
                    nc.tensor.matmul(mlp_ps[:, 0:SETCOLS], weight, data, start=True, stop=True)\
                      .then_inc(mlp_product, 1)

                def radial(i, b, part):
                    g = i * 2 + b
                    if part == 0:
                        pe.wait_ge(mlp_active, g * 3 + 3)
                        if not first(g, 2):
                            pe.wait_ge(prod_ready, g - 1)
                    for c in ((0,), (1, 2))[part]:
                        last = nc.tensor.matmul(radial_ps[:, b, 2 * c:2 * c + 2, :], hid3[:, b, c * P:(c + 1) * P],
                                                m4[:, :, :], start=True, stop=True)
                    if part == 1:
                        last.then_inc(radial_ready, 1)

                def segment_sum(i, b):
                    g = i * 2 + b
                    pe.wait_ge(prod_ready, g + 1)
                    if not first(g):
                        pe.wait_ge(added, g)
                    for t in range(G):
                        s, v = prod[:, b, t], shot[:, b, t]
                        o = sum_ps[:, :, 0:W]
                        nc.tensor.matmul(o[:, 0, :], s[:, 0].rearrange("p h c -> p (h c)"), v[:, 0, :],
                                         start=t == 0, stop=False, skip_group_check=True)
                        nc.tensor.matmul(o[:, 1:4:2, :], s[:, 1].rearrange("p h c -> p (h c)"), v[:, 0:4:2, :],
                                         start=False, stop=False, skip_group_check=True)
                        nc.tensor.matmul(o[:, 2:4, :], s[:, 2].rearrange("p h c -> p (h c)"), v[:, 0:4:3, :],
                                         start=False, stop=False, skip_group_check=True)
                        last = nc.tensor.matmul(o[:, 0:3, :], s[:, 3].rearrange("p h c -> p (h c)"), v[:, 1:4, :],
                                                start=False, stop=t == G - 1, skip_group_check=True)
                    last.then_inc(summed, 1)

                def step(i, b, first=False, last=False):
                    after = (i, 1) if b == 0 else (i + 1, 0)
                    before = (i - 1, 1) if b == 0 else (i, 0)
                    if not last:
                        layer(*after, 0)
                    radial(i, b, 0)
                    if not last:
                        layer(*after, 1)
                    radial(i, b, 1)
                    if not last:
                        layer(*after, 2)
                    if not first:
                        segment_sum(*before)

                for n in range(3):
                    layer(0, 0, n)
                step(0, 0, first=True)
                step(0, 1)
                with pe.Fori(1, GROUPS // 2 - 1) as i:
                    for b in range(2):
                        step(i, b)
                step(GROUPS // 2 - 1, 0)
                step(GROUPS // 2 - 1, 1, last=True)
                segment_sum(GROUPS // 2 - 1, 1)

        for s in [*per_pass]:
            nc.gpsimd.sem_clear(s)
        with nc.Block() as block:
            @block.vector
            def _(dve):
                nc.vector.tensor_scalar(rel[:, :], rel[:, :], float(-W), None, ALU.add)
                nc.vector.tensor_scalar(start_row[:, :], start_row[:, :], float(W), float(N), ALU.add, ALU.min)


def window_prelude(nc, src, dst, sh, src_all, rel, sh_all, start_row, passes, columns, ident, sem):
    loaded = sem("dst_loaded")
    done = sem("window_step")
    transposed = sem("window_transposed")
    iota_made = sem("iota_made")
    blocks = GROUPS // TBLOCK
    with ExitStack() as ctx:
        dst_i = ctx.enter_context(nc.sbuf_tensor("dst_i", [P, TILES], i32))
        iota_i = ctx.enter_context(nc.sbuf_tensor("iota_i", [P, W], i32))
        low = ctx.enter_context(nc.sbuf_tensor("low", [P, GROUPS], f32))
        low_t = ctx.enter_context(nc.sbuf_tensor("low_t", [TBLOCK, 1], f32))
        low_b = ctx.enter_context(nc.sbuf_tensor("low_b", [TBLOCK, blocks, P], f32))
        start = ctx.enter_context(nc.sbuf_tensor("start", [P, GROUPS], f32))
        high = ctx.enter_context(nc.sbuf_tensor("high", [P, 1], f32))
        high_1 = ctx.enter_context(nc.sbuf_tensor("high_1", [1, 2], f32))
        high_i = ctx.enter_context(nc.sbuf_tensor("high_i", [1, 2], i32))
        ps = ctx.enter_context(nc.psum_tensor("window_ps", [P, 4, 512], f32))
        block = ctx.enter_context(nc.Block())

        @block.sync
        def _(sp):
            sp.dma_start(dst_i[:, :], dst).then_inc(loaded, 16)
            sp.dma_start(src_all[:, :], src).then_inc(loaded, 16)
            sp.dma_start(sh_all[:, :, :], sh).then_inc(loaded, 16)
            sp.wait_ge(loaded, 48)

        @block.gpsimd
        def _(pool):
            nc.gpsimd.iota(iota_i[:, :], pattern=[[1, W]], base=0, channel_multiplier=0).then_inc(iota_made, 1)

        @block.tensor
        def _(pe):
            pe.wait_ge(done, 2)
            for k in range(blocks):
                last = nc.tensor.transpose(ps[0:TBLOCK, k, 0:P], low[:, k * TBLOCK:(k + 1) * TBLOCK], ident[:, :])
            last.then_inc(transposed, 1)
            pe.wait_ge(done, 2 + 2 * blocks)
            for k in range(blocks):
                last = nc.tensor.matmul(ps[:, 3, k * TBLOCK:(k + 1) * TBLOCK], low_b[:, k, :],
                                        ident[0:TBLOCK, 0:TBLOCK], start=True, stop=True)
            last.then_inc(transposed, 1)
            pe.wait_ge(done, 2 + 2 * blocks + 4)
            nc.tensor.transpose(ps[0:1, 0, 0:P], high[:, 0:1], ident[:, :]).then_inc(transposed, 1)

        @block.vector
        def _(dve):
            count = [0]

            def step(ins):
                count[0] += 1
                ins.then_inc(done, 1)
                dve.wait_ge(done, count[0])

            dve.wait_ge(iota_made, 1)
            nc.vector.tensor_copy(columns[:, :], iota_i[:, :])
            dve.wait_ge(loaded, 48)
            step(nc.vector.tensor_copy(rel[:, :], dst_i[:, :]))
            step(nc.vector.tensor_reduce(low[:, :], rel[:, :].rearrange("p (g t) -> p g t", t=G), X, ALU.min))
            dve.wait_ge(transposed, 1)
            for k in range(blocks):
                step(nc.vector.tensor_reduce(low_t[:, :], ps[0:TBLOCK, k, 0:P], X, ALU.min))
                step(nc.vector.tensor_copy(low_b[:, k, :], low_t[:, :].broadcast_to([TBLOCK, P])))
            dve.wait_ge(transposed, 2)
            step(nc.vector.tensor_copy(start[:, :], ps[:, 3, 0:GROUPS]))
            step(nc.vector.tensor_copy(start_row[:, :], start[0:1, :]))
            rel3 = rel[:, :].rearrange("p (g t) -> p g t", t=G)
            step(nc.vector.tensor_tensor(rel3, rel3, start[:, :].unsqueeze(2).broadcast_to([P, GROUPS, G]),
                                         ALU.subtract))
            step(nc.vector.tensor_reduce(high[:, :], rel[:, :], X, ALU.max))
            dve.wait_ge(transposed, 3)
            step(nc.vector.tensor_reduce(high_1[:, 0:1], ps[0:1, 0, 0:P], X, ALU.max))
            step(nc.vector.tensor_copy(high_i[:, 0:1], high_1[:, 0:1]))
            step(nc.vector.tensor_scalar(high_i[:, 1:2], high_i[:, 0:1], W.bit_length() - 1, None,
                                         ALU.arith_shift_right))
            step(nc.vector.tensor_scalar(passes[:, :], high_i[:, 1:2], 1.0, None, ALU.add))


def node_phase(nc, ctx, x_sets, wts, wc0, wc1, gamma0, beta0, gamma1, ident, pair, eps, acc, out, sem):
    def sb(name, shape, dt=f32):
        return ctx.enter_context(nc.sbuf_tensor(name, shape, dt))

    x_all = sb("x_all", [P, COMP, HALF])
    o_all = sb("o_all", [P, COMP, HALF])
    sums = sb("sums", [P, 2, CHUNKS])
    tot = sb("tot", [P, 4])
    stat = sb("stat", [P, 12])
    x_loaded = sem("x_sets_loaded")
    dense_phase(nc, x_sets, wts, wc0, wc1, x_all, o_all, sums, acc, x_loaded, sem)
    norm_scales(nc, gamma0, beta0, gamma1, pair, eps, o_all, sums, tot, stat, sem)
    finish(nc, x_all, o_all, stat, ident, eps, out, sem)


def dense_phase(nc, x_sets, wts, wc0, wc1, x_all, o_all, sums, acc, x_loaded, sem):
    a_ready = sem("a_ready")
    a_read = sem("a_read")
    squares = sem("squares")
    lines = sem("lines")
    poly = sem("poly")
    b_ready = sem("b_ready")
    o_ready = sem("o_ready")
    o_moved = sem("o_moved")
    with ExitStack() as ctx:
        def sb(name, shape):
            return ctx.enter_context(nc.sbuf_tensor(name, shape, f32))

        sq = sb("sq", [P, COMP, CH])
        line = sb("line", [P, 2, CH])
        vv = sb("vv", [P, CH])
        q = sb("q", [P, 2, CH])
        basis = sb("basis", [P, COMP, CH])
        junk = sb("junk", [P, 3, CH])
        a_ps = ctx.enter_context(nc.psum_tensor("a_ps", [P, COMP, 512], f32))
        o_ps = ctx.enter_context(nc.psum_tensor("o_ps", [P, COMP, 512], f32))
        block = ctx.enter_context(nc.Block())

        @block.sync
        def _(sp):
            for k in range(COMP):
                sp.dma_start(x_all[:, k, :], x_sets[:, k, :]).then_inc(x_loaded, 16)

        @block.tensor
        def _(pe):
            pe.wait_ge(x_loaded, 16 * COMP)
            def step(j):
                if not first(j):
                    pe.wait_ge(a_read, j * 2)
                for k in range(COMP):
                    wa, wb = (LIN0_A, LIN0_B) if k == 0 else (LIN1_A, LIN1_B)
                    slot = max(k - 1, 0)
                    nc.tensor.matmul(a_ps[:, k, 0:CH], wts[:, wa, :], acc[:, slot, bass.ds(j * CH, CH)],
                                     start=True, stop=False)
                    last = nc.tensor.matmul(a_ps[:, k, 0:CH], wts[:, wb, :],
                                            acc[:, slot, bass.ds(j * CH + HALF, CH)], start=False, stop=True)
                last.then_inc(a_ready, 1)
                if not first(j):
                    pe.wait_ge(o_moved, j)
                for k in range(COMP):
                    nc.tensor.matmul(o_ps[:, k, 0:CH], wts[:, SC1D if k else SC0D, :],
                                     x_all[:, k, bass.ds(j * CH, CH)], start=True, stop=False)
                pe.wait_ge(b_ready, j + 1)
                for k in range(COMP):
                    last = nc.tensor.matmul(o_ps[:, k, 0:CH], wts[:, WB1D if k else WB0D, :], basis[:, k, :],
                                            start=False, stop=True)
                last.then_inc(o_ready, 1)

            step(0)
            with pe.Fori(1, CHUNKS) as j:
                step(j)

        @block.scalar
        def _(act):
            def step(j):
                act.wait_ge(a_ready, j + 1)
                if not first(j):
                    act.wait_ge(b_ready, j)
                nc.scalar.activation(sq[:, :, :], a_ps[:, :, 0:CH], ACT.Square).then_inc(squares, 1)
                nc.scalar.activation(line[:, 0, :], a_ps[:, 0, 0:CH], ACT.Identity, bias=wc0[:, 0:1],
                                     scale=wc0[:, 1:2])
                nc.scalar.activation(line[:, 1, :], a_ps[:, 0, 0:CH], ACT.Identity, bias=wc1[:, 0:1],
                                     scale=wc1[:, 1:2]).then_inc(a_read, 1)
                act.wait_ge(o_ready, j + 1)
                nc.scalar.activation(o_all[:, 0, bass.ds(j * CH, CH)], o_ps[:, 0, 0:CH], ACT.Identity,
                                     accum_out=sums[:, 0, bass.ds(j, 1)])
                nc.scalar.activation(o_all[:, 1:COMP, bass.ds(j * CH, CH)], o_ps[:, 1:COMP, 0:CH], ACT.Identity)
                if not first(j):
                    act.wait_ge(o_moved, j)
                nc.scalar.activation(junk[:, :, :], o_ps[:, 1:COMP, 0:CH], ACT.Square,
                                     accum_out=sums[:, 1, bass.ds(j, 1)]).then_inc(o_moved, 1)

            step(0)
            with act.Fori(1, CHUNKS) as j:
                step(j)

        @block.vector
        def _(dve):
            def step(j):
                dve.wait_ge(squares, j + 1)
                nc.vector.tensor_tensor(vv[:, :], sq[:, 1, :], sq[:, 2, :], ALU.add).then_inc(poly, 1)
                dve.wait_ge(poly, j * 5 + 1)
                nc.vector.tensor_tensor(vv[:, :], vv[:, :], sq[:, 3, :], ALU.add).then_inc(poly, 1)
                dve.wait_ge(a_read, j * 2 + 1)
                if not first(j):
                    dve.wait_ge(o_ready, j)
                nc.vector.scalar_tensor_tensor(q[:, 0, :], sq[:, 0, :], wc0[:, 3:4], line[:, 0, :], ALU.mult, ALU.add)
                nc.vector.scalar_tensor_tensor(q[:, 1, :], sq[:, 0, :], wc1[:, 2:3], line[:, 1, :], ALU.mult, ALU.add)\
                  .then_inc(poly, 1)
                dve.wait_ge(poly, j * 5 + 3)
                nc.vector.scalar_tensor_tensor(q[:, 0, :], vv[:, :], wc0[:, 4:5], q[:, 0, :], ALU.mult, ALU.add)
                nc.vector.scalar_tensor_tensor(q[:, 1, :], vv[:, :], wc1[:, 3:4], q[:, 1, :], ALU.mult, ALU.add)\
                  .then_inc(poly, 1)
                dve.wait_ge(poly, j * 5 + 4)
                nc.vector.tensor_tensor(q[:, 0, :], a_ps[:, 0, 0:CH], q[:, 0, :], ALU.mult).then_inc(poly, 1)
                nc.vector.tensor_tensor(basis[:, 1:COMP, :], a_ps[:, 1:COMP, 0:CH],
                                        q[:, 1, :].unsqueeze(1).broadcast_to([P, 3, CH]), ALU.mult)\
                  .then_inc(a_read, 1)
                dve.wait_ge(poly, j * 5 + 5)
                nc.vector.scalar_tensor_tensor(basis[:, 0, :], vv[:, :], wc0[:, 2:3], q[:, 0, :], ALU.mult, ALU.add)\
                  .then_inc(b_ready, 1)

            step(0)
            with dve.Fori(1, CHUNKS) as j:
                step(j)


MEAN_NEG, SCALE0, SHIFT0, SCALE1, T0, T1, T2, T3 = range(8)


def norm_scales(nc, gamma0, beta0, gamma1, pair, eps, o_all, sums, tot, stat, sem):
    dve_step = sem("scale_dve")
    pe_step = sem("scale_pe")
    act_step = sem("scale_act")
    with ExitStack() as ctx:
        part = ctx.enter_context(nc.sbuf_tensor("part", [P, 4], f32))
        junk = ctx.enter_context(nc.sbuf_tensor("square_junk", [P, HALF], f32))
        ps = ctx.enter_context(nc.psum_tensor("scale_ps", [P, 512], f32))
        block = ctx.enter_context(nc.Block())

        @block.vector
        def _(dve):
            count = [0]

            def step(ins):
                count[0] += 1
                ins.then_inc(dve_step, 1)
                dve.wait_ge(dve_step, count[0])

            step(nc.vector.tensor_reduce(part[:, 0:1], sums[:, 0, :], X, ALU.add))
            step(nc.vector.tensor_reduce(part[:, 1:2], sums[:, 1, :], X, ALU.add))
            dve.wait_ge(pe_step, 1)
            step(nc.vector.tensor_scalar(stat[:, MEAN_NEG:MEAN_NEG + 1], ps[:, 0:1], -1.0 / N, None, ALU.mult))
            step(nc.vector.tensor_scalar(stat[:, T0:T0 + 1], ps[:, 1:2], 1.0 / (3 * N), EPS, ALU.mult, ALU.add))
            dve.wait_ge(pe_step, 2)
            step(nc.vector.tensor_scalar(stat[:, T1:T1 + 1], ps[:, 2:3], 1.0 / N, EPS, ALU.mult, ALU.add))
            dve.wait_ge(act_step, 3)
            step(nc.vector.reciprocal(stat[:, T2:T2 + 2], tot[:, 0:2]))
            step(nc.vector.tensor_tensor(stat[:, SCALE0:SCALE0 + 1], stat[:, T3:T3 + 1], gamma0[:, :], ALU.mult))
            step(nc.vector.tensor_tensor(stat[:, SCALE1:SCALE1 + 1], stat[:, T2:T2 + 1], gamma1[:, :], ALU.mult))
            step(nc.vector.scalar_tensor_tensor(stat[:, SHIFT0:SHIFT0 + 1], stat[:, MEAN_NEG:MEAN_NEG + 1],
                                                stat[:, SCALE0:SCALE0 + 1], beta0[:, :], ALU.mult, ALU.add))

        @block.tensor
        def _(pe):
            pe.wait_ge(dve_step, 2)
            nc.tensor.matmul(ps[:, 0:2], pair[:, :], part[:, 0:2], start=True, stop=True).then_inc(pe_step, 1)
            pe.wait_ge(act_step, 2)
            pe.wait_ge(dve_step, 4)
            nc.tensor.matmul(ps[:, 2:3], pair[:, :], part[:, 2:3], start=True, stop=True).then_inc(pe_step, 1)

        @block.scalar
        def _(act):
            act.wait_ge(dve_step, 3)
            for lo, n in ((0, HALF), (C, N - HALF)):
                nc.scalar.activation(junk[lo:lo + C, 0:n], o_all[lo:lo + C, 0, 0:n], ACT.Square,
                                     bias=stat[lo:lo + C, MEAN_NEG:MEAN_NEG + 1],
                                     accum_out=part[lo:lo + C, 2:3]).then_inc(act_step, 1)
            act.wait_ge(dve_step, 5)
            nc.scalar.activation(tot[:, 0:2], stat[:, T0:T0 + 2], ACT.Sqrt).then_inc(act_step, 1)


def finish(nc, x_all, o_all, stat, ident, eps, out, sem):
    y_made = sem("y_made")
    y_turned = sem("y_turned")
    ln_step = sem("ln_step")
    ln_gate = sem("ln_gate")
    ln_root = sem("ln_root")
    ln_done = sem("ln_done")
    stored = [sem(f"out_stored{b}") for b in range(2)]
    scaled = sem("y0_scaled")
    with ExitStack() as ctx:
        y = ctx.enter_context(nc.sbuf_tensor("y", [P, COMP, P], f32))
        st = ctx.enter_context(nc.sbuf_tensor("st", [P, 2, 6], f32))
        mv = ctx.enter_context(nc.sbuf_tensor("mv", [P, 2, 2], f32))
        root = ctx.enter_context(nc.sbuf_tensor("root", [P, 2], f32))
        rstd = ctx.enter_context(nc.sbuf_tensor("rstd", [P, 2], f32))
        res = ctx.enter_context(nc.sbuf_tensor("res", [P, 2, F], f32))
        y_ps = ctx.enter_context(nc.psum_tensor("y_ps", [P, COMP, P], f32))
        block = ctx.enter_context(nc.Block())

        @block.vector
        def _(dve):
            def step(j):
                cols = bass.ds(j * P, P)
                nc.vector.tensor_scalar(y[:, 0, :], o_all[:, 0, cols], stat[:, SCALE0:SCALE0 + 1],
                                        stat[:, SHIFT0:SHIFT0 + 1], ALU.mult, ALU.add).then_inc(scaled, 1)
                nc.vector.scalar_tensor_tensor(y[:, 1:COMP, :], o_all[:, 1:COMP, cols], stat[:, SCALE1:SCALE1 + 1],
                                               x_all[:, 1:COMP, cols], ALU.mult, ALU.add)
                dve.wait_ge(scaled, j + 1)
                nc.vector.tensor_tensor(y[:, 0, :], y[:, 0, :], x_all[:, 0, cols], ALU.add).then_inc(y_made, 1)
                dve.wait_ge(y_turned, j + 1)
                for s in range(2):
                    nc.vector.bn_stats(st[:, s, :], y_ps[:, :, s * C:(s + 1) * C]).then_inc(ln_step, 1)
                dve.wait_ge(ln_step, j * 5 + 2)
                dve.sem_inc(ln_gate, 1)
                for s in range(2):
                    nc.vector.bn_aggr(mv[:, s, :], st[:, s, :]).then_inc(ln_step, 1)
                dve.wait_ge(ln_root, j + 1)
                nc.vector.reciprocal(rstd[:, :], root[:, :]).then_inc(ln_step, 1)
                dve.wait_ge(ln_step, j * 5 + 5)
                for s in range(2):
                    if not first(j):
                        dve.wait_ge(stored[s], j * 16)
                    nc.vector.tensor_scalar(res[:, s, 0:C], y_ps[:, 0, s * C:(s + 1) * C], mv[:, s, 0:1],
                                            rstd[:, s:s + 1], ALU.subtract, ALU.mult)
                    nc.vector.tensor_scalar(res[:, s, C:F].rearrange("p (c k) -> p k c", k=3),
                                            y_ps[:, 1:COMP, s * C:(s + 1) * C], mv[:, s, 0:1],
                                            rstd[:, s:s + 1], ALU.subtract, ALU.mult).then_inc(ln_done, 1)

            step(0)
            with dve.Fori(1, NTILES) as j:
                step(j)

        @block.scalar
        def _(act):
            def step(j):
                act.wait_ge(ln_step, j * 5 + 4)
                nc.scalar.activation(root[:, :], mv[:, :, 1], ACT.Sqrt, bias=eps[:, :]).then_inc(ln_root, 1)

            step(0)
            with act.Fori(1, NTILES) as j:
                step(j)

        @block.tensor
        def _(pe):
            def step(j):
                pe.wait_ge(y_made, j + 1)
                if not first(j):
                    pe.wait_ge(ln_done, j * 2)
                for k in range(COMP):
                    last = nc.tensor.transpose(y_ps[:, k, :], y[:, k, :], ident[:, :])
                last.then_inc(y_turned, 1)

            step(0)
            with pe.Fori(1, NTILES) as j:
                step(j)

        @block.sync
        def _(sp):
            def store(j, s, rows):
                sp.wait_ge(ln_done, j * 2 + s + 1)
                sp.dma_start(out[bass.ds(j * P + s * HALF, rows), :], res[0:rows, s, :]).then_inc(stored[s], 16)

            with sp.Fori(0, LAST_FULL) as j:
                for s in range(2):
                    store(j, s, P)
            store(LAST_FULL, 0, P)
            store(LAST_FULL, 1, LAST_ROWS)
            for j in range(LAST_FULL + 1, NTILES):
                store(j, 0, P)
                sp.wait_ge(ln_done, j * 2 + 2)
                sp.sem_inc(stored[1], 16)
            for s in range(2):
                sp.wait_ge(stored[s], 16 * NTILES)


def kernel(x, src, dst, edge_attr_16, edge_attr_4, **weights):
    import numpy as np
    import concourse.bacc as bacc
    from concourse.bass_utils import run_bass_kernel_spmd

    x, src, dst, edge_attr_16, edge_attr_4 = (np.asarray(a) for a in (x, src, dst, edge_attr_16, edge_attr_4))

    xp = np.zeros((NODES, F), x.dtype)
    xp[:N] = x
    comps = np.concatenate([xp[:, None, :C], xp[:, C:].reshape(NODES, C, 3).transpose(0, 2, 1)], 1)
    x_pairs = np.ascontiguousarray(comps.reshape(NODES, 2, 2 * C).transpose(2, 1, 0))
    x_sets = np.ascontiguousarray(comps.reshape(2, HALF, COMP, C).transpose(0, 3, 2, 1).reshape(P, COMP, HALF))

    def padded(a, fill):
        b = np.full((TILES * P, *a.shape[1:]), fill, a.dtype)
        b[:E] = a
        return b

    arrays = {
        "x_pairs": x_pairs,
        "x_sets": x_sets,
        "src": np.ascontiguousarray(padded(src, 0).reshape(TILES, P).T).view(np.uint32),
        "dst": np.ascontiguousarray(padded(dst, N).reshape(TILES, P).T),
        "sh": np.ascontiguousarray(padded(edge_attr_4, 0).reshape(TILES, P, COMP).transpose(1, 0, 2)),
        "rbf": np.ascontiguousarray(padded(edge_attr_16, 0).reshape(GROUPS, G // 2, 2, P, R)
                                    .transpose(0, 2, 4, 1, 3).reshape(GROUPS, 2 * R, SETCOLS)),
    }
    for name, a in weights.items():
        arrays[name.removeprefix("L0_gnn_")] = np.ascontiguousarray(a)

    nc = bacc.Bacc("TRN2", target_bir_lowering=False, num_devices=1)
    args = {name: nc.dram_tensor(f"in_{name}", a.shape, mybir.dt.from_np(a.dtype), kind="ExternalInput").ap()
            for name, a in arrays.items()}
    out = nc.dram_tensor("out", (N, F), f32, kind="ExternalOutput").ap()
    edge = {name: args.pop(name) for name in ("x_pairs", "x_sets", "src", "dst", "sh", "rbf")}
    build(nc, **edge, w=args, out=out)
    result = run_bass_kernel_spmd(nc, [{f"in_{name}": a for name, a in arrays.items()}], core_ids=[0])
    return result.results[0]["out"]
```

```python
from contextlib import ExitStack

import concourse.bass as bass
from concourse import mybir

P = 128
C = 64
COMP = 4
F = COMP * C
R = 16
N = 6250
E = 206250
G = 4
U = 4
W = 32
SETCOLS = G // 2 * P
GROUPS = -(-E // (U * G * P)) * U
TILES = GROUPS * G
HALF = -(-N // (2 * P)) * P
NODES = 2 * HALF
CH = 320
CHUNKS = HALF // CH
UPT = 5
UPCHUNKS = NODES // (UPT * P)
NTILES = HALF // P
ACCW = NODES + W
EPS = 1e-5
TBLOCK = 101
assert HALF % CH == 0 and CHUNKS % 2 == 0 and UPCHUNKS % 2 == 0 and GROUPS % TBLOCK == 0
LAST_FULL = (N - HALF) // P
LAST_ROWS = N - HALF - LAST_FULL * P

(UP_A, UP_B, M2D, M3D, WB0D, WB1D, SC0D, SC1D, LIN0_A, LIN0_B, LIN1HI_A, LIN1HI_B, LIN1LO_A,
 LIN1LO_B) = range(14)

f32 = mybir.dt.float32
f32r = mybir.dt.float32r
i32 = mybir.dt.int32
u32 = mybir.dt.uint32
ALU = mybir.AluOpType
ACT = mybir.ActivationFunctionType
X = mybir.AxisListType.X


def first(step, count=1):
    return isinstance(step, int) and step < count


def following(i, b, count=1):
    return (i, b + count) if b + count < U else (i + 1, b + count - U)


def preceding(i, b, count=1):
    return (i, b - count) if b >= count else (i - 1, b - count + U)


SCHEDULE = (
    ((0, 0, 0), (1, 0, 1), (0, 1, 2), (1, 1, 3), (0, 2, 2), (1, 2, 3), (0, 3, 2), (1, 3, 3)),
    ((2, 0, 0), (3, 0, 1), (2, 1, 2), (3, 1, 3),
     (2, 3, 0), (3, 3, 1), (2, 2, 2), (3, 2, 3)),
)
STARTS = SCHEDULE[0][:4]
STOPS = SCHEDULE[1][-4:]


def build(nc, x_pairs, x_sets, src, dst, sh, rbf, w, out):
    up_table = nc.dram_tensor("up_table", (NODES, F), f32, kind="Internal").ap()

    with ExitStack() as whole:
        def sb(name, shape, dt=f32, ctx=whole):
            return ctx.enter_context(nc.sbuf_tensor(name, shape, dt))

        def sem(name):
            return whole.enter_context(nc.semaphore(name))

        wts = sb("wts", [P, 14, P])
        m1d = sb("m1d", [2 * R, P])
        m4 = [sb("m4_high", [P, F], f32r), sb("m4_low", [P, F], f32r)]
        wc0 = sb("wc0", [P, 5])
        wc1 = sb("wc1", [P, 4])
        gamma0 = sb("gamma0", [P, 1])
        beta0 = sb("beta0", [P, 1])
        gamma1 = sb("gamma1", [P, 1])
        ident = sb("ident", [P, P])
        pair = sb("pair", [P, P])
        eps = sb("eps", [P, 1])
        fold = sb("fold", [P, W])
        acc = sb("acc", [P, 2, ACCW])

        load_weights(nc, w, wts, m1d, m4, wc0, wc1, gamma0, beta0, gamma1, ident, pair, fold, eps, acc, sem)
        project_nodes(nc, x_pairs, wts, up_table, sem)
        with ExitStack() as edges:
            edge_phase(nc, edges, src, dst, sh, rbf, up_table, m1d, m4, wts, ident, fold, acc, sem)
        with ExitStack() as nodes:
            node_phase(nc, nodes, x_sets, wts, wc0, wc1, gamma0, beta0, gamma1, ident, pair, eps, acc, out, sem)


def load_weights(nc, w, wts, m1d, m4, wc0, wc1, gamma0, beta0, gamma1, ident, pair, fold, eps, acc, sem):
    cleared = sem("weights_cleared")
    pool_cleared = sem("constants_cleared")
    made = sem("constants_made")
    loaded = sem("weights_loaded")
    scaled = sem("m4_scaled")
    rounded = sem("m4_rounded")
    lo, hi = slice(0, C), slice(C, 2 * C)
    with nc.sbuf_tensor("m4_whole", [P, F], f32) as m4_whole, nc.Block() as block:
        @block.vector
        def _(dve):
            nc.vector.memset(wts[:, :, :], 0.0).then_inc(cleared, 1)
            nc.vector.memset(m1d[:, :], 0.0).then_inc(cleared, 1)
            nc.vector.memset(eps[:, :], EPS)
            nc.vector.memset(acc[:, :, :], 0.0)
            dve.wait_ge(loaded, 16 * 36)
            nc.vector.tensor_scalar(m4_whole[:, 3 * C:4 * C], m4_whole[:, 3 * C:4 * C], 3.0 ** -0.5, None,
                                    ALU.mult).then_inc(scaled, 1)
            dve.wait_ge(scaled, 1)
            nc.vector.tensor_copy(m4[0][:, :], m4_whole[:, :]).then_inc(rounded, 1)
            dve.wait_ge(rounded, 1)
            nc.vector.tensor_tensor(m4[1][:, :], m4_whole[:, :], m4[0][:, :].bitcast(f32), ALU.subtract)

        @block.gpsimd
        def _(pool):
            nc.gpsimd.memset(ident[:, :], 0.0).then_inc(pool_cleared, 1)
            nc.gpsimd.memset(pair[:, :], 0.0).then_inc(pool_cleared, 1)
            nc.gpsimd.memset(fold[:, :], 0.0).then_inc(pool_cleared, 1)
            pool.wait_ge(pool_cleared, 3)
            nc.gpsimd.affine_select(out=ident[:, :], in_=ident[:, :], compare_op=ALU.not_equal, fill=1.0,
                                    base=0, pattern=[[-1, P]], channel_multiplier=1).then_inc(made, 1)
            for n, shift in enumerate((0, C, -C)):
                nc.gpsimd.affine_select(out=pair[:, :], in_=pair[:, :], compare_op=ALU.not_equal, fill=1.0,
                                        base=shift, pattern=[[-1, P]], channel_multiplier=1).then_inc(made, 1)
                pool.wait_ge(made, n + 2)
            for q in range(P // W):
                nc.gpsimd.affine_select(out=fold[:, :], in_=fold[:, :], compare_op=ALU.not_equal, fill=1.0,
                                        base=-W * q, pattern=[[-1, W]], channel_multiplier=1).then_inc(made, 1)
                pool.wait_ge(made, q + 5)

        def put(eng, dst, src):
            eng.dma_start(dst, src).then_inc(loaded, 16)

        @block.sync
        def _(sp):
            sp.wait_ge(cleared, 2)
            for tile, a, b in ((UP_A, "W_up0", "W_up1"), (UP_B, "W_up1", "W_up1"), (M2D, "M2", "M2"),
                               (M3D, "M3", "M3"), (WB0D, "WB0", "WB0"), (WB1D, "WB1", "WB1"),
                               (SC0D, "Wsc0", "Wsc0"), (SC1D, "Wsc1", "Wsc1")):
                put(sp, wts[lo, tile, lo], w[a])
                put(sp, wts[hi, tile, hi], w[b])
            put(sp, m1d[0:R, lo], w["M1"])
            put(sp, m1d[R:2 * R, hi], w["M1"])

        @block.scalar
        def _(act):
            act.wait_ge(cleared, 2)
            put(act, wts[lo, LIN0_A, lo], w["W_lin0"])
            put(act, wts[lo, LIN0_B, hi], w["W_lin0"])
            put(act, wts[hi, LIN1HI_A, lo], w["W_lin1"])
            put(act, wts[hi, LIN1HI_B, hi], w["W_lin1"])
            put(act, wts[lo, LIN1LO_A, lo], w["W_lin1"])
            put(act, wts[lo, LIN1LO_B, hi], w["W_lin1"])
            put(act, m4_whole[lo, :], w["M4"])
            put(act, m4_whole[hi, :], w["M4"])
            for half in (lo, hi):
                put(act, wc0[half, :], w["Wc0"])
                put(act, wc1[half, :], w["Wc1"])
            for half in (lo, hi):
                put(act, gamma0[half, :], w["gamma0"].rearrange("(c a) -> c a", a=1))
                put(act, beta0[half, :], w["beta0"].rearrange("(c a) -> c a", a=1))
            put(act, gamma1[lo, :], w["gamma1"].rearrange("(c a) -> c a", a=1))

            put(act, gamma1[hi, :], w["gamma1"].rearrange("(c a) -> c a", a=1))


def project_nodes(nc, x_pairs, wts, up_table, sem):
    loaded = [sem(f"x_loaded{b}") for b in range(2)]
    stored = [sem(f"up_stored{b}") for b in range(2)]
    product = sem("up_product")
    moved = sem("up_moved")
    with ExitStack() as ctx:
        xin = ctx.enter_context(nc.sbuf_tensor("xin", [P, 2, 2, UPT * P], f32))
        up_out = ctx.enter_context(nc.sbuf_tensor("up_out", [P, 2, UPT, F], f32))
        up_ps = ctx.enter_context(nc.psum_tensor("up_ps", [P, 2, UPT + 1, F], f32))
        rows = up_table.rearrange("(n p) f -> p n f", p=P)
        block = ctx.enter_context(nc.Block())

        @block.sync
        def _(sp):
            def load(i, b):
                if not first(i):
                    sp.wait_ge(product, i * 2 + b - 1)
                sp.dma_start(xin[:, b, :, :], x_pairs[:, :, bass.ds((i * 2 + b) * (UPT * P), UPT * P)])\
                  .then_inc(loaded[b], 16)

            for b in range(2):
                load(0, b)
            with sp.Fori(1, UPCHUNKS // 2) as i:
                for b in range(2):
                    load(i, b)

        @block.tensor
        def _(pe):
            def multiply(i, b):
                pe.wait_ge(loaded[b], i * 16 + 16)
                if not first(i):
                    pe.wait_ge(moved, i * 2 + b - 1)
                for t in range(UPT):
                    nc.tensor.matmul(up_ps[:, b, t, 0:P], xin[:, b, 0, t * P:(t + 1) * P],
                                     wts[:, UP_A, :], start=True, stop=True)
                    last = nc.tensor.matmul(up_ps[:, b, t, P:2 * P], xin[:, b, 1, t * P:(t + 1) * P],
                                            wts[:, UP_B, :], start=True, stop=True)
                last.then_inc(product, 1)

            for b in range(2):
                multiply(0, b)
            with pe.Fori(1, UPCHUNKS // 2) as i:
                for b in range(2):
                    multiply(i, b)

        @block.vector
        def _(dve):
            def step(i):
                for b in range(2):
                    if not first(i):
                        dve.wait_ge(stored[b], i * 16)
                    dve.wait_ge(product, i * 2 + b + 1)
                    nc.vector.tensor_copy(up_out[:, b, :, :], up_ps[:, b, 0:UPT, :]).then_inc(moved, 1)

            step(0)
            with dve.Fori(1, UPCHUNKS // 2) as i:
                step(i)

        @block.scalar
        def _(act):
            def step(i):
                for b in range(2):
                    act.wait_ge(moved, i * 2 + b + 1)
                    act.dma_start(rows[:, bass.ds((i * 2 + b) * UPT, UPT), :], up_out[:, b, :, :])\
                       .then_inc(stored[b], 16)

            step(0)
            with act.Fori(1, UPCHUNKS // 2) as i:
                step(i)
            for b in range(2):
                act.wait_ge(stored[b], 16 * (UPCHUNKS // 2))


def edge_phase(nc, ctx, src, dst, sh, rbf, up_table, m1d, m4, wts, ident, fold, acc, sem):
    def sb(name, shape, dt=f32):
        return ctx.enter_context(nc.sbuf_tensor(name, shape, dt))

    src_all = sb("src_all", [P, TILES], u32)
    rel = sb("rel", [P, TILES])
    sh_all = sb("sh_all", [P, TILES, COMP])
    start_row = sb("start_row", [1, GROUPS], i32)
    passes = sb("passes", [1, 1], i32)
    columns = sb("columns", [P, W])

    window_prelude(nc, src, dst, sh, src_all, rel, sh_all, start_row, passes, columns, ident, sem)

    idx = sb("idx", [P, U, G], u32)
    rbf_t = sb("rbf_t", [2 * R, 2, SETCOLS])
    hid = sb("hid", [P, 2, SETCOLS])
    whole = sb("whole", [C, 2, 2, SETCOLS])
    parts = sb("parts", [P, 2, 2, SETCOLS], f32r)
    xg = sb("xg", [P, U, G, F])
    prod = sb("prod", [P, 2, G, 8, C])
    onehot = sb("onehot", [P, 2, G, W])
    shot = sb("shot", [P, U, G, COMP, W])
    quarters = sb("quarters", [P, 2, F])
    mlp_ps = ctx.enter_context(nc.psum_tensor("mlp_ps", [P, 2, 512], f32))
    radial_ps = ctx.enter_context(nc.psum_tensor("radial_ps", [P, 2, G, F], f32))
    sum_ps = ctx.enter_context(nc.psum_tensor("sum_ps", [P, 2, 512], f32))
    folded_ps = sum_ps[:, :, F:F + 2 * W].rearrange("p b (h w) -> p b h w", h=2)

    rbf_loaded = [sem(f"rbf_loaded{b}") for b in range(2)]
    gathered = [sem(f"gathered{b}") for b in range(U)]
    idx_staged = sem("idx_staged")
    gather_gate = sem("gather_gate")
    mlp_product = sem("mlp_product")
    mlp_active = sem("mlp_active")
    split = sem("split")
    radial_ready = sem("radial_ready")
    onehot_made = sem("onehot_made")
    shot_made = sem("shot_made")
    prod_ready = sem("prod_ready")
    summed = sem("summed")
    moved = sem("moved")
    folded = sem("folded")
    added = sem("added")
    per_pass = [*rbf_loaded, idx_staged, gather_gate, mlp_product, mlp_active, split, radial_ready,
                onehot_made, shot_made, prod_ready, summed, moved, folded, added]

    n_passes = nc.values_load(passes[0:1, 0:1], min_val=1, max_val=N // W + 1)
    with nc.Fori(0, n_passes) as k:
        earlier = k * (16 * G * (GROUPS // U))
        with nc.Block() as block:
            @block.sync
            def _(sp):
                def load(i, b):
                    g = i * U + b
                    if not first(g, 2):
                        sp.wait_ge(mlp_product, (g - 2) * 3 + 1)
                    sp.dma_start(rbf_t[:, b % 2, :], rbf[bass.ds(g, 1), :, :].rearrange("a r c -> r (a c)"))\
                      .then_inc(rbf_loaded[b % 2], 16)

                for b in range(U):
                    load(0, b)
                with sp.Fori(1, GROUPS // U) as i:
                    for b in range(U):
                        load(i, b)

            @block.scalar
            def _(act):
                def stage(i, b):
                    nc.scalar.copy(idx[:, b, :], src_all[:, bass.ds((i * U + b) * G, G)]).then_inc(idx_staged, 1)

                def hidden(i, b, layer):
                    act.wait_ge(mlp_product, (i * U + b) * 3 + layer + 1)
                    if layer < 2:
                        nc.scalar.activation(hid[:, layer, :], mlp_ps[:, b % 2, 0:SETCOLS], ACT.Silu)\
                          .then_inc(mlp_active, 1)
                        return
                    for s in range(2):
                        pre = mlp_ps[s * C:(s + 1) * C, b % 2, 0:SETCOLS]
                        nc.scalar.activation(parts[0:C, b % 2, s, :], pre, ACT.Silu)
                        last = nc.scalar.activation(whole[:, b % 2, s, :], pre, ACT.Silu)
                    last.then_inc(mlp_active, 1)

                def move(i, b):
                    g = i * U + b
                    act.wait_ge(summed, g + 1)
                    if not first(g, 2):
                        act.wait_ge(folded, g - 1)
                    nc.scalar.activation(quarters[:, b % 2, :], sum_ps[:, b % 2, 0:F], ACT.Identity)\
                      .then_inc(moved, 1)

                def step(i, b, to_stage=True, to_hide=True):
                    if to_hide:
                        for layer in range(2):
                            hidden(*following(i, b, 2), layer)
                    if to_stage:
                        act.wait_ge(gathered[b], earlier + (i + 1) * (16 * G))
                        stage(i + 1, b)
                    if to_hide:
                        hidden(*following(i, b, 2), 2)
                    if not first(i * U + b):
                        move(*preceding(i, b))

                for b in range(U):
                    stage(0, b)
                for b in range(2):
                    for layer in range(3):
                        hidden(0, b, layer)
                for b in range(U):
                    step(0, b)
                with act.Fori(1, GROUPS // U - 1) as i:
                    for b in range(U):
                        step(i, b)
                for b in range(U):
                    step(GROUPS // U - 1, b, to_stage=False, to_hide=b < U - 2)
                move(GROUPS // U - 1, U - 1)

            @block.gpsimd
            def _(pool):
                def gather(b):
                    for t in range(G):
                        nc.gpsimd.indirect_dma_start(
                            out=xg[:, b, t, :], out_offset=None, in_=up_table[:, :],
                            in_offset=bass.IndirectOffsetOnAxis(ap=idx[:, b, t:t + 1], axis=0))\
                          .then_inc(gathered[b], 16)

                for b in range(U):
                    pool.wait_ge(idx_staged, b + 1)
                    gather(b)
                with pool.Fori(1, GROUPS // U) as i:
                    for b in range(U):
                        pool.wait_ge(prod_ready, i * U + b - U + 1)
                        pool.wait_ge(idx_staged, i * U + b + 1)
                        pool.sem_inc(gather_gate, 1)
                        gather(b)

            @block.vector
            def _(dve):
                def low_parts(i, b):
                    dve.wait_ge(mlp_active, (i * U + b) * 3 + 3)
                    nc.vector.tensor_tensor(parts[C:P, b % 2], whole[:, b % 2], parts[0:C, b % 2].bitcast(f32),
                                            ALU.subtract).then_inc(split, 1)

                def onehots(i, b):
                    g = i * U + b
                    if not first(g, 2):
                        dve.wait_ge(shot_made, g - 1)
                    nc.vector.tensor_tensor(
                        onehot[:, b % 2, :, :], columns[:, :].unsqueeze(1).broadcast_to([P, G, W]),
                        rel[:, bass.ds(g * G, G)].unsqueeze(2).broadcast_to([P, G, W]), ALU.is_equal)\
                      .then_inc(onehot_made, 1)

                def harmonics(i, b):
                    g = i * U + b
                    dve.wait_ge(onehot_made, g + 1)
                    if not first(g, U):
                        dve.wait_ge(summed, g - U + 1)
                    nc.vector.tensor_tensor(
                        shot[:, b, :, :, :], onehot[:, b % 2, :, :].unsqueeze(2).broadcast_to([P, G, COMP, W]),
                        sh_all[:, bass.ds(g * G, G), :].unsqueeze(3).broadcast_to([P, G, COMP, W]), ALU.mult)\
                      .then_inc(shot_made, 1)

                def products(i, b):
                    g = i * U + b
                    if not first(g, 2):
                        dve.wait_ge(summed, g - 1)
                    dve.wait_ge(radial_ready, i * U + b + 1)
                    dve.wait_ge(gathered[b], earlier + (i + 1) * (16 * G))
                    rad, rows, o = radial_ps[:, b % 2], xg[:, b], prod[:, b % 2]
                    vector_rows = rows[:, :, C:F].rearrange("p t (s c) -> p t s c", c=C)
                    nc.vector.tensor_tensor(
                        o[:, :, 0:5:4, :], rad[:, :, 0:2 * C].rearrange("p t (s c) -> p t s c", c=C),
                        rows[:, :, 0:C].unsqueeze(2).broadcast_to([P, G, 2, C]), ALU.mult)
                    nc.vector.tensor_tensor(
                        o[:, :, 1:4, :], rad[:, :, 2 * C:3 * C].unsqueeze(2).broadcast_to([P, G, 3, C]),
                        vector_rows, ALU.mult)
                    nc.vector.tensor_tensor(
                        o[:, :, 5:8, :], rad[:, :, 3 * C:F].unsqueeze(2).broadcast_to([P, G, 3, C]),
                        vector_rows, ALU.mult).then_inc(prod_ready, 1)

                def add(i, b):
                    g = i * U + b
                    start = dve.value_load(start_row[0:1, bass.ds(g, 1)], min_val=0, max_val=N)
                    dve.wait_ge(folded, g + 1)
                    if not first(g):
                        dve.wait_ge(added, g)
                    window = acc[:, :, bass.ds(start, W)]
                    nc.vector.tensor_tensor(window, folded_ps[:, b % 2], window, ALU.add).then_inc(added, 1)

                def step(i, b, last=False):
                    harmonics(i, b)
                    if not last:
                        low_parts(*following(i, b))
                    products(i, b)
                    if not last:
                        onehots(*following(i, b))
                    if not first(i * U + b, 2):
                        add(*preceding(i, b, 2))

                low_parts(0, 0)
                onehots(0, 0)
                for b in range(U):
                    step(0, b)
                with dve.Fori(1, GROUPS // U - 1) as i:
                    for b in range(U):
                        step(i, b)
                for b in range(U):
                    step(GROUPS // U - 1, b, last=b == U - 1)
                for b in range(U - 2, U):
                    add(GROUPS // U - 1, b)

            @block.tensor
            def _(pe):
                def layer(i, b, n):
                    g = i * U + b
                    if n == 0:
                        pe.wait_ge(rbf_loaded[b % 2], i * (8 * U) + (b // 2 + 1) * 16)
                        if not first(g, 2):
                            pe.wait_ge(mlp_active, (g - 1) * 3)
                    else:
                        pe.wait_ge(mlp_active, g * 3 + n)
                    weight = (m1d[:, :], wts[:, M2D, :], wts[:, M3D, :])[n]
                    data = (rbf_t[:, b % 2, :], hid[:, 0, :], hid[:, 1, :])[n]
                    nc.tensor.matmul(mlp_ps[:, b % 2, 0:SETCOLS], weight, data, start=True, stop=True)\
                      .then_inc(mlp_product, 1)

                def radial(i, b):
                    g = i * U + b
                    pe.wait_ge(split, g + 1)
                    if not first(g, 2):
                        pe.wait_ge(prod_ready, g - 1)
                    for t in range(G):
                        s, c = divmod(t, G // 2)
                        for n in range(2):
                            last = nc.tensor.matmul(radial_ps[:, b % 2, t, :],
                                                    parts[:, b % 2, s, c * P:(c + 1) * P], m4[n][:, :],
                                                    start=n == 0, stop=n == 1)
                    last.then_inc(radial_ready, 1)

                def segment_sum(i, b, part):
                    g = i * U + b
                    if part == 0:
                        pe.wait_ge(prod_ready, g + 1)
                        if not first(g, 2):
                            pe.wait_ge(added, g - 1)
                    for tile, harmonic, quarter in SCHEDULE[part]:
                        o = sum_ps[quarter * W:(quarter + 1) * W, b % 2, 0:F]
                        terms = prod[:, b % 2, tile]
                        if harmonic == 0:
                            terms = terms[:, 0:4, :]
                        else:
                            o = o.rearrange("n (s c) -> n s c", c=C)[:, 0:harmonic + 1:harmonic, :]
                            terms = terms[:, 4 + harmonic:3:-harmonic, :]
                        last = nc.tensor.matmul(o, shot[:, b, tile, harmonic, :], terms,
                                                start=(tile, harmonic, quarter) in STARTS,
                                                stop=(tile, harmonic, quarter) in STOPS, skip_group_check=True)
                    if part == 1:
                        last.then_inc(summed, 1)

                def folding(i, b):
                    pe.wait_ge(moved, i * U + b + 1)
                    for h in range(2):
                        last = nc.tensor.matmul(folded_ps[:, b % 2, h, :], quarters[:, b % 2, h * P:(h + 1) * P],
                                                fold[:, :], start=True, stop=True)
                    last.then_inc(folded, 1)

                def step(i, b, last=False):
                    g = i * U + b
                    for n in range(3):
                        if not last:
                            layer(*following(i, b, 2), n)
                        if n == 0:
                            radial(i, b)
                        if n == 1 and not first(g, 2):
                            folding(*preceding(i, b, 2))
                        if n and not first(g):
                            segment_sum(*preceding(i, b), n - 1)

                for b in range(2):
                    for n in range(3):
                        layer(0, b, n)
                for b in range(U):
                    step(0, b)
                with pe.Fori(1, GROUPS // U - 1) as i:
                    for b in range(U):
                        step(i, b)
                for b in range(U):
                    step(GROUPS // U - 1, b, last=b >= U - 2)
                for part in range(2):
                    segment_sum(GROUPS // U - 1, U - 1, part)
                for b in range(U - 2, U):
                    folding(GROUPS // U - 1, b)

        for s in [*per_pass]:
            nc.gpsimd.sem_clear(s)
        with nc.Block() as block:
            @block.vector
            def _(dve):
                nc.vector.tensor_scalar(rel[:, :], rel[:, :], float(-W), None, ALU.add)
                nc.vector.tensor_scalar(start_row[:, :], start_row[:, :], float(W), float(N), ALU.add, ALU.min)


def window_prelude(nc, src, dst, sh, src_all, rel, sh_all, start_row, passes, columns, ident, sem):
    loaded = sem("dst_loaded")
    done = sem("window_step")
    transposed = sem("window_transposed")
    iota_made = sem("iota_made")
    blocks = GROUPS // TBLOCK
    with ExitStack() as ctx:
        dst_i = ctx.enter_context(nc.sbuf_tensor("dst_i", [P, TILES], i32))
        iota_i = ctx.enter_context(nc.sbuf_tensor("iota_i", [P, W], i32))
        low = ctx.enter_context(nc.sbuf_tensor("low", [P, GROUPS], f32))
        low_t = ctx.enter_context(nc.sbuf_tensor("low_t", [TBLOCK, 1], f32))
        low_b = ctx.enter_context(nc.sbuf_tensor("low_b", [TBLOCK, blocks, P], f32))
        start = ctx.enter_context(nc.sbuf_tensor("start", [P, GROUPS], f32))
        high = ctx.enter_context(nc.sbuf_tensor("high", [P, 1], f32))
        high_1 = ctx.enter_context(nc.sbuf_tensor("high_1", [1, 2], f32))
        high_i = ctx.enter_context(nc.sbuf_tensor("high_i", [1, 2], i32))
        ps = ctx.enter_context(nc.psum_tensor("window_ps", [P, 5, 512], f32))
        block = ctx.enter_context(nc.Block())

        @block.sync
        def _(sp):
            sp.dma_start(dst_i[:, :], dst).then_inc(loaded, 16)
            sp.dma_start(src_all[:, :], src).then_inc(loaded, 16)
            sp.dma_start(sh_all[:, :, :], sh).then_inc(loaded, 16)
            sp.wait_ge(loaded, 48)

        @block.gpsimd
        def _(pool):
            nc.gpsimd.iota(iota_i[:, :], pattern=[[1, W]], base=0, channel_multiplier=0).then_inc(iota_made, 1)

        @block.tensor
        def _(pe):
            pe.wait_ge(done, 2)
            for k in range(blocks):
                last = nc.tensor.transpose(ps[0:TBLOCK, k, 0:P], low[:, k * TBLOCK:(k + 1) * TBLOCK], ident[:, :])
            last.then_inc(transposed, 1)
            pe.wait_ge(done, 2 + 2 * blocks)
            for k in range(blocks):
                last = nc.tensor.matmul(ps[:, 4, k * TBLOCK:(k + 1) * TBLOCK], low_b[:, k, :],
                                        ident[0:TBLOCK, 0:TBLOCK], start=True, stop=True)
            last.then_inc(transposed, 1)
            pe.wait_ge(done, 2 + 2 * blocks + 4)
            nc.tensor.transpose(ps[0:1, 0, 0:P], high[:, 0:1], ident[:, :]).then_inc(transposed, 1)

        @block.vector
        def _(dve):
            count = [0]

            def step(ins):
                count[0] += 1
                ins.then_inc(done, 1)
                dve.wait_ge(done, count[0])

            dve.wait_ge(iota_made, 1)
            nc.vector.tensor_copy(columns[:, :], iota_i[:, :])
            dve.wait_ge(loaded, 48)
            step(nc.vector.tensor_copy(rel[:, :], dst_i[:, :]))
            step(nc.vector.tensor_reduce(low[:, :], rel[:, :].rearrange("p (g t) -> p g t", t=G), X, ALU.min))
            dve.wait_ge(transposed, 1)
            for k in range(blocks):
                step(nc.vector.tensor_reduce(low_t[:, :], ps[0:TBLOCK, k, 0:P], X, ALU.min))
                step(nc.vector.tensor_copy(low_b[:, k, :], low_t[:, :].broadcast_to([TBLOCK, P])))
            dve.wait_ge(transposed, 2)
            step(nc.vector.tensor_copy(start[:, :], ps[:, 4, 0:GROUPS]))
            step(nc.vector.tensor_copy(start_row[:, :], start[0:1, :]))
            rel3 = rel[:, :].rearrange("p (g t) -> p g t", t=G)
            step(nc.vector.tensor_tensor(rel3, rel3, start[:, :].unsqueeze(2).broadcast_to([P, GROUPS, G]),
                                         ALU.subtract))
            step(nc.vector.tensor_reduce(high[:, :], rel[:, :], X, ALU.max))
            dve.wait_ge(transposed, 3)
            step(nc.vector.tensor_reduce(high_1[:, 0:1], ps[0:1, 0, 0:P], X, ALU.max))
            step(nc.vector.tensor_copy(high_i[:, 0:1], high_1[:, 0:1]))
            step(nc.vector.tensor_scalar(high_i[:, 1:2], high_i[:, 0:1], W.bit_length() - 1, None,
                                         ALU.arith_shift_right))
            step(nc.vector.tensor_scalar(passes[:, :], high_i[:, 1:2], 1.0, None, ALU.add))


def node_phase(nc, ctx, x_sets, wts, wc0, wc1, gamma0, beta0, gamma1, ident, pair, eps, acc, out, sem):
    def sb(name, shape, dt=f32):
        return ctx.enter_context(nc.sbuf_tensor(name, shape, dt))

    x_all = sb("x_all", [P, COMP, HALF])
    o_all = sb("o_all", [P, COMP, HALF])
    sums = sb("sums", [P, 2, CHUNKS])
    tot = sb("tot", [P, 4])
    stat = sb("stat", [P, 12])
    x_loaded = sem("x_sets_loaded")
    dense_phase(nc, x_sets, wts, wc0, wc1, x_all, o_all, sums, acc, x_loaded, sem)
    norm_scales(nc, gamma0, beta0, gamma1, pair, eps, o_all, sums, tot, stat, sem)
    finish(nc, x_all, o_all, stat, ident, eps, out, sem)


def dense_phase(nc, x_sets, wts, wc0, wc1, x_all, o_all, sums, acc, x_loaded, sem):
    a_ready = sem("a_ready")
    a_read = sem("a_read")
    squares = sem("squares")
    lines = sem("lines")
    poly = sem("poly")
    b_ready = sem("b_ready")
    o_ready = sem("o_ready")
    o_moved = sem("o_moved")
    with ExitStack() as ctx:
        def sb(name, shape):
            return ctx.enter_context(nc.sbuf_tensor(name, shape, f32))

        sq = sb("sq", [P, COMP, CH])
        line = sb("line", [P, 2, CH])
        vv = sb("vv", [P, CH])
        q = sb("q", [P, 2, CH])
        basis = sb("basis", [P, COMP, CH])
        junk = sb("junk", [P, 3, CH])
        a_ps = ctx.enter_context(nc.psum_tensor("a_ps", [P, COMP, 512], f32))
        o_ps = ctx.enter_context(nc.psum_tensor("o_ps", [P, COMP, 512], f32))
        block = ctx.enter_context(nc.Block())

        @block.sync
        def _(sp):
            for k in range(COMP):
                sp.dma_start(x_all[:, k, :], x_sets[:, k, :]).then_inc(x_loaded, 16)

        @block.tensor
        def _(pe):
            pe.wait_ge(x_loaded, 16 * COMP)
            def step(j):
                if not first(j):
                    pe.wait_ge(a_read, j * 2)
                for k in range(COMP):
                    wa, wb = ((LIN0_A, LIN0_B), (LIN1HI_A, LIN1HI_B), (LIN1LO_A, LIN1LO_B),
                              (LIN1HI_A, LIN1HI_B))[k]
                    slot = k // 2
                    nc.tensor.matmul(a_ps[:, k, 0:CH], wts[:, wa, :], acc[:, slot, bass.ds(j * CH, CH)],
                                     start=True, stop=False)
                    last = nc.tensor.matmul(a_ps[:, k, 0:CH], wts[:, wb, :],
                                            acc[:, slot, bass.ds(j * CH + HALF, CH)], start=False, stop=True)
                last.then_inc(a_ready, 1)
                if not first(j):
                    pe.wait_ge(o_moved, j)
                for k in range(COMP):
                    nc.tensor.matmul(o_ps[:, k, 0:CH], wts[:, SC1D if k else SC0D, :],
                                     x_all[:, k, bass.ds(j * CH, CH)], start=True, stop=False)
                pe.wait_ge(b_ready, j + 1)
                for k in range(COMP):
                    last = nc.tensor.matmul(o_ps[:, k, 0:CH], wts[:, WB1D if k else WB0D, :], basis[:, k, :],
                                            start=False, stop=True)
                last.then_inc(o_ready, 1)

            step(0)
            with pe.Fori(1, CHUNKS) as j:
                step(j)

        @block.scalar
        def _(act):
            def step(j):
                act.wait_ge(a_ready, j + 1)
                if not first(j):
                    act.wait_ge(b_ready, j)
                nc.scalar.activation(sq[:, :, :], a_ps[:, :, 0:CH], ACT.Square).then_inc(squares, 1)
                nc.scalar.activation(line[:, 0, :], a_ps[:, 0, 0:CH], ACT.Identity, bias=wc0[:, 0:1],
                                     scale=wc0[:, 1:2])
                nc.scalar.activation(line[:, 1, :], a_ps[:, 0, 0:CH], ACT.Identity, bias=wc1[:, 0:1],
                                     scale=wc1[:, 1:2]).then_inc(a_read, 1)
                act.wait_ge(o_ready, j + 1)
                nc.scalar.activation(o_all[:, 0, bass.ds(j * CH, CH)], o_ps[:, 0, 0:CH], ACT.Identity,
                                     accum_out=sums[:, 0, bass.ds(j, 1)])
                nc.scalar.activation(o_all[:, 1:COMP, bass.ds(j * CH, CH)], o_ps[:, 1:COMP, 0:CH], ACT.Identity)
                if not first(j):
                    act.wait_ge(o_moved, j)
                nc.scalar.activation(junk[:, :, :], o_ps[:, 1:COMP, 0:CH], ACT.Square,
                                     accum_out=sums[:, 1, bass.ds(j, 1)]).then_inc(o_moved, 1)

            step(0)
            with act.Fori(1, CHUNKS) as j:
                step(j)

        @block.vector
        def _(dve):
            def step(j):
                dve.wait_ge(squares, j + 1)
                nc.vector.tensor_tensor(vv[:, :], sq[:, 1, :], sq[:, 2, :], ALU.add).then_inc(poly, 1)
                dve.wait_ge(poly, j * 5 + 1)
                nc.vector.tensor_tensor(vv[:, :], vv[:, :], sq[:, 3, :], ALU.add).then_inc(poly, 1)
                dve.wait_ge(a_read, j * 2 + 1)
                if not first(j):
                    dve.wait_ge(o_ready, j)
                nc.vector.scalar_tensor_tensor(q[:, 0, :], sq[:, 0, :], wc0[:, 3:4], line[:, 0, :], ALU.mult, ALU.add)
                nc.vector.scalar_tensor_tensor(q[:, 1, :], sq[:, 0, :], wc1[:, 2:3], line[:, 1, :], ALU.mult, ALU.add)\
                  .then_inc(poly, 1)
                dve.wait_ge(poly, j * 5 + 3)
                nc.vector.scalar_tensor_tensor(q[:, 0, :], vv[:, :], wc0[:, 4:5], q[:, 0, :], ALU.mult, ALU.add)
                nc.vector.scalar_tensor_tensor(q[:, 1, :], vv[:, :], wc1[:, 3:4], q[:, 1, :], ALU.mult, ALU.add)\
                  .then_inc(poly, 1)
                dve.wait_ge(poly, j * 5 + 4)
                nc.vector.tensor_tensor(q[:, 0, :], a_ps[:, 0, 0:CH], q[:, 0, :], ALU.mult).then_inc(poly, 1)
                nc.vector.tensor_tensor(basis[:, 1:COMP, :], a_ps[:, 1:COMP, 0:CH],
                                        q[:, 1, :].unsqueeze(1).broadcast_to([P, 3, CH]), ALU.mult)\
                  .then_inc(a_read, 1)
                dve.wait_ge(poly, j * 5 + 5)
                nc.vector.scalar_tensor_tensor(basis[:, 0, :], vv[:, :], wc0[:, 2:3], q[:, 0, :], ALU.mult, ALU.add)\
                  .then_inc(b_ready, 1)

            step(0)
            with dve.Fori(1, CHUNKS) as j:
                step(j)


MEAN_NEG, SCALE0, SHIFT0, SCALE1, T0, T1, T2, T3 = range(8)


def norm_scales(nc, gamma0, beta0, gamma1, pair, eps, o_all, sums, tot, stat, sem):
    dve_step = sem("scale_dve")
    pe_step = sem("scale_pe")
    act_step = sem("scale_act")
    with ExitStack() as ctx:
        part = ctx.enter_context(nc.sbuf_tensor("part", [P, 4], f32))
        junk = ctx.enter_context(nc.sbuf_tensor("square_junk", [P, HALF], f32))
        ps = ctx.enter_context(nc.psum_tensor("scale_ps", [P, 512], f32))
        block = ctx.enter_context(nc.Block())

        @block.vector
        def _(dve):
            count = [0]

            def step(ins):
                count[0] += 1
                ins.then_inc(dve_step, 1)
                dve.wait_ge(dve_step, count[0])

            step(nc.vector.tensor_reduce(part[:, 0:1], sums[:, 0, :], X, ALU.add))
            step(nc.vector.tensor_reduce(part[:, 1:2], sums[:, 1, :], X, ALU.add))
            dve.wait_ge(pe_step, 1)
            step(nc.vector.tensor_scalar(stat[:, MEAN_NEG:MEAN_NEG + 1], ps[:, 0:1], -1.0 / N, None, ALU.mult))
            step(nc.vector.tensor_scalar(stat[:, T0:T0 + 1], ps[:, 1:2], 1.0 / (3 * N), EPS, ALU.mult, ALU.add))
            dve.wait_ge(pe_step, 2)
            step(nc.vector.tensor_scalar(stat[:, T1:T1 + 1], ps[:, 2:3], 1.0 / N, EPS, ALU.mult, ALU.add))
            dve.wait_ge(act_step, 3)
            step(nc.vector.reciprocal(stat[:, T2:T2 + 2], tot[:, 0:2]))
            step(nc.vector.tensor_tensor(stat[:, SCALE0:SCALE0 + 1], stat[:, T3:T3 + 1], gamma0[:, :], ALU.mult))
            step(nc.vector.tensor_tensor(stat[:, SCALE1:SCALE1 + 1], stat[:, T2:T2 + 1], gamma1[:, :], ALU.mult))
            step(nc.vector.scalar_tensor_tensor(stat[:, SHIFT0:SHIFT0 + 1], stat[:, MEAN_NEG:MEAN_NEG + 1],
                                                stat[:, SCALE0:SCALE0 + 1], beta0[:, :], ALU.mult, ALU.add))

        @block.tensor
        def _(pe):
            pe.wait_ge(dve_step, 2)
            nc.tensor.matmul(ps[:, 0:2], pair[:, :], part[:, 0:2], start=True, stop=True).then_inc(pe_step, 1)
            pe.wait_ge(act_step, 2)
            pe.wait_ge(dve_step, 4)
            nc.tensor.matmul(ps[:, 2:3], pair[:, :], part[:, 2:3], start=True, stop=True).then_inc(pe_step, 1)

        @block.scalar
        def _(act):
            act.wait_ge(dve_step, 3)
            for lo, n in ((0, HALF), (C, N - HALF)):
                nc.scalar.activation(junk[lo:lo + C, 0:n], o_all[lo:lo + C, 0, 0:n], ACT.Square,
                                     bias=stat[lo:lo + C, MEAN_NEG:MEAN_NEG + 1],
                                     accum_out=part[lo:lo + C, 2:3]).then_inc(act_step, 1)
            act.wait_ge(dve_step, 5)
            nc.scalar.activation(tot[:, 0:2], stat[:, T0:T0 + 2], ACT.Sqrt).then_inc(act_step, 1)


def finish(nc, x_all, o_all, stat, ident, eps, out, sem):
    y_made = sem("y_made")
    y_turned = sem("y_turned")
    ln_step = sem("ln_step")
    ln_gate = sem("ln_gate")
    ln_root = sem("ln_root")
    ln_done = sem("ln_done")
    stored = [sem(f"out_stored{b}") for b in range(2)]
    scaled = sem("y0_scaled")
    with ExitStack() as ctx:
        y = ctx.enter_context(nc.sbuf_tensor("y", [P, COMP, P], f32))
        st = ctx.enter_context(nc.sbuf_tensor("st", [P, 2, 6], f32))
        mv = ctx.enter_context(nc.sbuf_tensor("mv", [P, 2, 2], f32))
        root = ctx.enter_context(nc.sbuf_tensor("root", [P, 2], f32))
        rstd = ctx.enter_context(nc.sbuf_tensor("rstd", [P, 2], f32))
        res = ctx.enter_context(nc.sbuf_tensor("res", [P, 2, F], f32))
        y_ps = ctx.enter_context(nc.psum_tensor("y_ps", [P, COMP, P], f32))
        block = ctx.enter_context(nc.Block())

        @block.vector
        def _(dve):
            def step(j):
                cols = bass.ds(j * P, P)
                nc.vector.tensor_scalar(y[:, 0, :], o_all[:, 0, cols], stat[:, SCALE0:SCALE0 + 1],
                                        stat[:, SHIFT0:SHIFT0 + 1], ALU.mult, ALU.add).then_inc(scaled, 1)
                nc.vector.scalar_tensor_tensor(y[:, 1:COMP, :], o_all[:, 1:COMP, cols], stat[:, SCALE1:SCALE1 + 1],
                                               x_all[:, 1:COMP, cols], ALU.mult, ALU.add)
                dve.wait_ge(scaled, j + 1)
                nc.vector.tensor_tensor(y[:, 0, :], y[:, 0, :], x_all[:, 0, cols], ALU.add).then_inc(y_made, 1)
                dve.wait_ge(y_turned, j + 1)
                for s in range(2):
                    nc.vector.bn_stats(st[:, s, :], y_ps[:, :, s * C:(s + 1) * C]).then_inc(ln_step, 1)
                dve.wait_ge(ln_step, j * 5 + 2)
                dve.sem_inc(ln_gate, 1)
                for s in range(2):
                    nc.vector.bn_aggr(mv[:, s, :], st[:, s, :]).then_inc(ln_step, 1)
                dve.wait_ge(ln_root, j + 1)
                nc.vector.reciprocal(rstd[:, :], root[:, :]).then_inc(ln_step, 1)
                dve.wait_ge(ln_step, j * 5 + 5)
                for s in range(2):
                    if not first(j):
                        dve.wait_ge(stored[s], j * 16)
                    nc.vector.tensor_scalar(res[:, s, 0:C], y_ps[:, 0, s * C:(s + 1) * C], mv[:, s, 0:1],
                                            rstd[:, s:s + 1], ALU.subtract, ALU.mult)
                    nc.vector.tensor_scalar(res[:, s, C:F].rearrange("p (c k) -> p k c", k=3),
                                            y_ps[:, 1:COMP, s * C:(s + 1) * C], mv[:, s, 0:1],
                                            rstd[:, s:s + 1], ALU.subtract, ALU.mult).then_inc(ln_done, 1)

            step(0)
            with dve.Fori(1, NTILES) as j:
                step(j)

        @block.scalar
        def _(act):
            def step(j):
                act.wait_ge(ln_step, j * 5 + 4)
                nc.scalar.activation(root[:, :], mv[:, :, 1], ACT.Sqrt, bias=eps[:, :]).then_inc(ln_root, 1)

            step(0)
            with act.Fori(1, NTILES) as j:
                step(j)

        @block.tensor
        def _(pe):
            def step(j):
                pe.wait_ge(y_made, j + 1)
                if not first(j):
                    pe.wait_ge(ln_done, j * 2)
                for k in range(COMP):
                    last = nc.tensor.transpose(y_ps[:, k, :], y[:, k, :], ident[:, :])
                last.then_inc(y_turned, 1)

            step(0)
            with pe.Fori(1, NTILES) as j:
                step(j)

        @block.sync
        def _(sp):
            def store(j, s, rows):
                sp.wait_ge(ln_done, j * 2 + s + 1)
                sp.dma_start(out[bass.ds(j * P + s * HALF, rows), :], res[0:rows, s, :]).then_inc(stored[s], 16)

            with sp.Fori(0, LAST_FULL) as j:
                for s in range(2):
                    store(j, s, P)
            store(LAST_FULL, 0, P)
            store(LAST_FULL, 1, LAST_ROWS)
            for j in range(LAST_FULL + 1, NTILES):
                store(j, 0, P)
                sp.wait_ge(ln_done, j * 2 + 2)
                sp.sem_inc(stored[1], 16)
            for s in range(2):
                sp.wait_ge(stored[s], 16 * NTILES)


def kernel(x, src, dst, edge_attr_16, edge_attr_4, **weights):
    import numpy as np
    import concourse.bacc as bacc
    from concourse.bass_utils import run_bass_kernel_spmd

    x, src, dst, edge_attr_16, edge_attr_4 = (np.asarray(a) for a in (x, src, dst, edge_attr_16, edge_attr_4))

    xp = np.zeros((NODES, F), x.dtype)
    xp[:N] = x
    comps = np.concatenate([xp[:, None, :C], xp[:, C:].reshape(NODES, C, 3).transpose(0, 2, 1)], 1)
    x_pairs = np.ascontiguousarray(comps.reshape(NODES, 2, 2 * C).transpose(2, 1, 0))
    x_sets = np.ascontiguousarray(comps.reshape(2, HALF, COMP, C).transpose(0, 3, 2, 1).reshape(P, COMP, HALF))

    def padded(a, fill):
        b = np.full((TILES * P, *a.shape[1:]), fill, a.dtype)
        b[:E] = a
        return b

    arrays = {
        "x_pairs": x_pairs,
        "x_sets": x_sets,
        "src": np.ascontiguousarray(padded(src, 0).reshape(TILES, P).T).view(np.uint32),
        "dst": np.ascontiguousarray(padded(dst, N).reshape(TILES, P).T),
        "sh": np.ascontiguousarray(padded(edge_attr_4, 0).reshape(TILES, P, COMP).transpose(1, 0, 2)),
        "rbf": np.ascontiguousarray(padded(edge_attr_16, 0).reshape(GROUPS, 2, SETCOLS, R)
                                    .transpose(0, 1, 3, 2).reshape(GROUPS, 2 * R, SETCOLS)),
    }
    for name, a in weights.items():
        arrays[name.removeprefix("L0_gnn_")] = np.ascontiguousarray(a)

    nc = bacc.Bacc("TRN2", target_bir_lowering=False, num_devices=1)
    args = {name: nc.dram_tensor(f"in_{name}", a.shape, mybir.dt.from_np(a.dtype), kind="ExternalInput").ap()
            for name, a in arrays.items()}
    out = nc.dram_tensor("out", (N, F), f32, kind="ExternalOutput").ap()
    edge = {name: args.pop(name) for name in ("x_pairs", "x_sets", "src", "dst", "sh", "rbf")}
    build(nc, **edge, w=args, out=out)
    result = run_bass_kernel_spmd(nc, [{f"in_{name}": a for name, a in arrays.items()}], core_ids=[0])
    return result.results[0]["out"]
```

```python
from contextlib import ExitStack

import concourse.bass as bass
from concourse import mybir

P = 128
C = 64
COMP = 4
F = COMP * C
R = 16
N = 6250
E = 206250
G = 4
U = 4
W = 32
SETCOLS = G // 2 * P
GROUPS = -(-E // (U * G * P)) * U
TILES = GROUPS * G
HALF = -(-N // (2 * P)) * P
NODES = 2 * HALF
CH = 200
CHUNKS = HALF // CH
UPT = 5
UPCHUNKS = NODES // (UPT * P)
NTILES = HALF // P
RING = 5
ACCW = NODES + W
EPS = 1e-5
TBLOCK = 101
assert HALF % CH == 0 and NTILES % RING == 0 and CHUNKS % 2 == 0 and UPCHUNKS % 2 == 0 and GROUPS % TBLOCK == 0
LAST_FULL = (N - HALF) // P
LAST_ROWS = N - HALF - LAST_FULL * P

UP_A, UP_B, M2D, M3D, WB0D, WB1D, SC0D, SC1D, LIN0_LO, LIN1_LO, LIN1_HI = range(11)

f32 = mybir.dt.float32
f32r = mybir.dt.float32r
i32 = mybir.dt.int32
u32 = mybir.dt.uint32
ALU = mybir.AluOpType
ACT = mybir.ActivationFunctionType
X = mybir.AxisListType.X


def first(step, count=1):
    return isinstance(step, int) and step < count


def following(i, b, count=1):
    return (i, b + count) if b + count < U else (i + 1, b + count - U)


def step_at(i, b, d, unroll):
    return i + (b + d) // unroll, (b + d) % unroll


def preceding(i, b, count=1):
    return (i, b - count) if b >= count else (i - 1, b - count + U)


SCHEDULE = (
    ((0, 0, 0), (1, 0, 1), (0, 1, 2), (1, 1, 3), (0, 2, 2), (1, 2, 3), (0, 3, 2), (1, 3, 3)),
    ((2, 0, 0), (3, 0, 1), (2, 1, 2), (3, 1, 3),
     (2, 3, 0), (3, 3, 1), (2, 2, 2), (3, 2, 3)),
)
STARTS = SCHEDULE[0][:4]
STOPS = SCHEDULE[1][-4:]


def build(nc, x_pairs, x_sets, src, dst, sh, rbf, w, out):
    up_table = nc.dram_tensor("up_table", (NODES, F), f32, kind="Internal").ap()

    with ExitStack() as whole:
        def sb(name, shape, dt=f32, ctx=whole):
            return ctx.enter_context(nc.sbuf_tensor(name, shape, dt))

        def sem(name):
            return whole.enter_context(nc.semaphore(name))

        wts = sb("wts", [P, 11, P])
        m1d = sb("m1d", [2 * R, P])
        m4 = [sb("m4_high", [P, F], f32r), sb("m4_low", [P, F], f32r)]
        wc0 = sb("wc0", [P, 5])
        wc1 = sb("wc1", [P, 4])
        gamma0 = sb("gamma0", [P, 1])
        beta0 = sb("beta0", [P, 1])
        gamma1 = sb("gamma1", [P, 1])
        ident = sb("ident", [P, P])
        pair = sb("pair", [P, P])
        eps = sb("eps", [P, 1])
        fold = sb("fold", [P, W])
        acc = sb("acc", [P, 2, ACCW])

        x_all = sb("x_all", [P, COMP, HALF])

        with ExitStack() as edges:
            src_all = sb("src_all", [P, TILES], u32, edges)
            rel = sb("rel", [P, TILES], f32, edges)
            sh_all = sb("sh_all", [P, TILES, COMP], f32, edges)
            start_row = sb("start_row", [1, GROUPS], i32, edges)
            passes = sb("passes", [1, 1], i32, edges)
            columns = sb("columns", [P, W], f32, edges)
            rbf_first = sb("rbf_first", [2 * R, 2, SETCOLS], f32, edges)
            sh_loaded = sem("sh_loaded")
            prepare(nc, w, x_pairs, src, dst, sh, rbf, rbf_first, wts, m1d, m4, wc0, wc1, gamma0, beta0, gamma1, ident, pair,
                    fold, eps, acc, up_table, src_all, rel, sh_all, start_row, passes, columns, sh_loaded, sem)
            edge_phase(nc, edges, rbf, rbf_first, x_sets, x_all, up_table, m1d, m4, wts, fold, acc, src_all, rel, sh_all,
                       start_row, passes, columns, sh_loaded, sem)
        with ExitStack() as nodes:
            node_phase(nc, nodes, x_all, wts, wc0, wc1, gamma0, beta0, gamma1, ident, pair, eps, acc, out, sem)


def prepare(nc, w, x_pairs, src, dst, sh, rbf, rbf_first, wts, m1d, m4, wc0, wc1, gamma0, beta0, gamma1, ident, pair, fold, eps,
            acc, up_table, src_all, rel, sh_all, start_row, passes, columns, sh_loaded, sem):
    up_cleared = sem("up_weights_cleared")
    cleared = sem("weights_cleared")
    zeroed = sem("constants_zeroed")
    made = sem("constants_made")
    iota_made = sem("iota_made")
    up_weights = sem("up_weights_loaded")
    weights = sem("weights_loaded")
    scaled = sem("m4_scaled")
    rounded = sem("m4_rounded")
    x_loaded = [sem(f"x_loaded{b}") for b in range(2)]
    stored = [sem(f"up_stored{b}") for b in range(2)]
    product = sem("up_product")
    moved = sem("up_moved")
    dst_loaded = sem("dst_loaded")
    src_loaded = sem("src_loaded")
    done = sem("window_step")
    transposed = sem("window_transposed")
    blocks = GROUPS // TBLOCK
    lo, hi = slice(0, C), slice(C, 2 * C)
    LOWEST, SPREAD, HIGHEST = 2, 4, 8
    with ExitStack() as ctx:
        def sb(name, shape, dt=f32):
            return ctx.enter_context(nc.sbuf_tensor(name, shape, dt))

        m4_whole = sb("m4_whole", [P, F])
        xin = sb("xin", [P, 2, 2, UPT * P])
        up_out = sb("up_out", [P, 2, UPT, F])
        dst_i = sb("dst_i", [P, TILES], i32)
        iota_i = sb("iota_i", [P, W], i32)
        low = sb("low", [P, GROUPS])
        low_t = sb("low_t", [TBLOCK, blocks])
        low_b = sb("low_b", [TBLOCK, blocks, P])
        start = sb("start", [P, GROUPS])
        high = sb("high", [P, 1])
        high_1 = sb("high_1", [1, 1])
        high_i = sb("high_i", [1, 2], i32)
        up_ps = ctx.enter_context(nc.psum_tensor("up_ps", [P, 2, UPT + 1, F], f32))
        window_ps = ctx.enter_context(nc.psum_tensor("window_ps", [P, 2, 512], f32))
        rows = up_table.rearrange("(n p) f -> p n f", p=P)
        block = ctx.enter_context(nc.Block())

        @block.sync
        def _(sp):
            def load(i, b):
                if not first(i):
                    sp.wait_ge(product, i * 2 + b - 1)
                sp.dma_start(xin[:, b, :, :], x_pairs[:, :, bass.ds((i * 2 + b) * (UPT * P), UPT * P)])\
                  .then_inc(x_loaded[b], 16)

            sp.wait_ge(up_cleared, 1)
            for tile, a, b in ((UP_A, "W_up0", "W_up1"), (UP_B, "W_up1", "W_up1")):
                sp.dma_start(wts[lo, tile, lo], w[a]).then_inc(up_weights, 16)
                sp.dma_start(wts[hi, tile, hi], w[b]).then_inc(up_weights, 16)
            load(0, 0)
            sp.dma_start(dst_i[:, :], dst).then_inc(dst_loaded, 16)
            load(0, 1)
            with sp.Fori(1, UPCHUNKS // 2) as i:
                for b in range(2):
                    load(i, b)
            sp.dma_start(src_all[:, :], src).then_inc(src_loaded, 16)
            for g in range(2):
                sp.dma_start(rbf_first[:, g, :], rbf[g]).then_inc(src_loaded, 16)
            sp.wait_ge(src_loaded, 48)

        @block.tensor
        def _(pe):
            def multiply(i, b):
                pe.wait_ge(x_loaded[b], i * 16 + 16)
                if not first(i):
                    pe.wait_ge(moved, i * 2 + b - 1)
                for t in range(UPT):
                    nc.tensor.matmul(up_ps[:, b, t, 0:P], xin[:, b, 0, t * P:(t + 1) * P],
                                     wts[:, UP_A, :], start=True, stop=True)
                    last = nc.tensor.matmul(up_ps[:, b, t, P:2 * P], xin[:, b, 1, t * P:(t + 1) * P],
                                            wts[:, UP_B, :], start=True, stop=True)
                last.then_inc(product, 1)

            pe.wait_ge(up_weights, 64)
            for b in range(2):
                multiply(0, b)
            pe.wait_ge(made, 1)
            pe.wait_ge(done, LOWEST)
            for k in range(blocks):
                last = nc.tensor.transpose(window_ps[0:TBLOCK, 0, k * P:(k + 1) * P],
                                           low[:, k * TBLOCK:(k + 1) * TBLOCK], ident[:, :])
            last.then_inc(transposed, 1)
            for b in range(2):
                multiply(1, b)
            pe.wait_ge(done, SPREAD)
            for k in range(blocks):
                last = nc.tensor.matmul(window_ps[:, 1, k * TBLOCK:(k + 1) * TBLOCK], low_b[:, k, :],
                                        ident[0:TBLOCK, 0:TBLOCK], start=True, stop=True)
            last.then_inc(transposed, 1)
            with pe.Fori(2, UPCHUNKS // 2) as i:
                for b in range(2):
                    multiply(i, b)
            pe.wait_ge(done, HIGHEST)
            nc.tensor.transpose(window_ps[0:1, 0, 0:P], high[:, 0:1], ident[:, :]).then_inc(transposed, 1)

        @block.scalar
        def _(act):
            def step(i):
                for b in range(2):
                    if not first(i):
                        act.wait_ge(stored[b], i * 16)
                    act.wait_ge(product, i * 2 + b + 1)
                    nc.scalar.activation(up_out[:, b, :, :], up_ps[:, b, 0:UPT, :], ACT.Identity).then_inc(moved, 1)
                    act.wait_ge(moved, i * 2 + b + 1)
                    act.dma_start(rows[:, bass.ds((i * 2 + b) * UPT, UPT), :], up_out[:, b, :, :])\
                       .then_inc(stored[b], 16)

            step(0)
            with act.Fori(1, UPCHUNKS // 2) as i:
                step(i)
            act.dma_start(sh_all[:, :, :], sh).then_inc(sh_loaded, 16)
            for b in range(2):
                act.wait_ge(stored[b], 16 * (UPCHUNKS // 2))

        @block.gpsimd
        def _(pool):
            nc.gpsimd.iota(iota_i[:, :], pattern=[[1, W]], base=0, channel_multiplier=0).then_inc(iota_made, 1)
            nc.gpsimd.memset(ident[:, :], 0.0).then_inc(zeroed, 1)
            nc.gpsimd.memset(pair[:, :], 0.0).then_inc(zeroed, 1)
            nc.gpsimd.memset(fold[:, :], 0.0).then_inc(zeroed, 1)
            pool.wait_ge(zeroed, 3)
            nc.gpsimd.affine_select(out=ident[:, :], in_=ident[:, :], compare_op=ALU.not_equal, fill=1.0,
                                    base=0, pattern=[[-1, P]], channel_multiplier=1).then_inc(made, 1)
            pool.wait_ge(cleared, 2)

            def put(dst, src):
                pool.dma_start(dst, src).then_inc(weights, 16)

            put(m4_whole[lo, :], w["M4"])
            put(m4_whole[hi, :], w["M4"])
            put(m1d[0:R, lo], w["M1"])
            put(m1d[R:2 * R, hi], w["M1"])
            for tile, name in ((M2D, "M2"), (M3D, "M3"), (WB0D, "WB0"), (WB1D, "WB1"), (SC0D, "Wsc0"),
                               (SC1D, "Wsc1")):
                put(wts[lo, tile, lo], w[name])
                put(wts[hi, tile, hi], w[name])
            put(wts[lo, LIN0_LO, lo], w["W_lin0"])
            put(wts[lo, LIN1_LO, lo], w["W_lin1"])
            put(wts[hi, LIN1_HI, lo], w["W_lin1"])
            for half in (lo, hi):
                put(wc0[half, :], w["Wc0"])
                put(wc1[half, :], w["Wc1"])
                for column, name in ((gamma0, "gamma0"), (beta0, "beta0"), (gamma1, "gamma1")):
                    put(column[half, :], w[name].rearrange("(c a) -> c a", a=1))
            for n, shift in enumerate((0, C, -C)):
                nc.gpsimd.affine_select(out=pair[:, :], in_=pair[:, :], compare_op=ALU.not_equal, fill=1.0,
                                        base=shift, pattern=[[-1, P]], channel_multiplier=1).then_inc(made, 1)
                pool.wait_ge(made, n + 2)
            for n in range(P // W):
                nc.gpsimd.affine_select(out=fold[:, :], in_=fold[:, :], compare_op=ALU.not_equal, fill=1.0,
                                        base=-W * n, pattern=[[-1, W]], channel_multiplier=1).then_inc(made, 1)
                pool.wait_ge(made, n + 5)

        @block.vector
        def _(dve):
            count = [0]

            def step(ins):
                count[0] += 1
                ins.then_inc(done, 1)
                dve.wait_ge(done, count[0])

            nc.vector.memset(wts[:, UP_A:UP_B + 1, :], 0.0).then_inc(up_cleared, 1)
            nc.vector.memset(wts[:, UP_B + 1:, :], 0.0).then_inc(cleared, 1)
            nc.vector.memset(m1d[:, :], 0.0).then_inc(cleared, 1)
            nc.vector.memset(eps[:, :], EPS)
            dve.wait_ge(iota_made, 1)
            nc.vector.tensor_copy(columns[:, :], iota_i[:, :])
            dve.wait_ge(dst_loaded, 16)
            step(nc.vector.tensor_copy(rel[:, :], dst_i[:, :]))
            step(nc.vector.tensor_reduce(low[:, :], rel[:, :].rearrange("p (g t) -> p g t", t=G), X, ALU.min))
            assert count[0] == LOWEST
            dve.wait_ge(transposed, 1)
            step(nc.vector.tensor_reduce(low_t[:, :],
                                         window_ps[0:TBLOCK, 0, :].rearrange("g (k p) -> g k p", p=P), X, ALU.min))
            step(nc.vector.tensor_copy(low_b[:, :, :], low_t[:, :].unsqueeze(2).broadcast_to([TBLOCK, blocks, P])))
            assert count[0] == SPREAD
            nc.vector.memset(acc[:, :, :], 0.0)
            dve.wait_ge(transposed, 2)
            step(nc.vector.tensor_copy(start[:, :], window_ps[:, 1, 0:GROUPS]))
            step(nc.vector.tensor_copy(start_row[:, :], start[0:1, :]))
            rel3 = rel[:, :].rearrange("p (g t) -> p g t", t=G)
            step(nc.vector.tensor_tensor(rel3, rel3, start[:, :].unsqueeze(2).broadcast_to([P, GROUPS, G]),
                                         ALU.subtract))
            step(nc.vector.tensor_reduce(high[:, :], rel[:, :], X, ALU.max))
            assert count[0] == HIGHEST
            dve.wait_ge(weights, 16 * 29)
            nc.vector.tensor_scalar(m4_whole[:, 3 * C:4 * C], m4_whole[:, 3 * C:4 * C], 3.0 ** -0.5, None,
                                    ALU.mult).then_inc(scaled, 1)
            dve.wait_ge(scaled, 1)
            nc.vector.tensor_copy(m4[0][:, :], m4_whole[:, :]).then_inc(rounded, 1)
            dve.wait_ge(rounded, 1)
            nc.vector.tensor_tensor(m4[1][:, :], m4_whole[:, :], m4[0][:, :].bitcast(f32), ALU.subtract)
            dve.wait_ge(transposed, 3)
            step(nc.vector.tensor_reduce(high_1[:, :], window_ps[0:1, 0, 0:P], X, ALU.max))
            step(nc.vector.tensor_copy(high_i[:, 0:1], high_1[:, :]))
            step(nc.vector.tensor_scalar(high_i[:, 1:2], high_i[:, 0:1], W.bit_length() - 1, None,
                                         ALU.arith_shift_right))
            step(nc.vector.tensor_scalar(passes[:, :], high_i[:, 1:2], 1.0, None, ALU.add))


def edge_phase(nc, ctx, rbf, rbf_first, x_sets, x_all, up_table, m1d, m4, wts, fold, acc, src_all, rel, sh_all, start_row,
               passes, columns, sh_loaded, sem):
    def sb(name, shape, dt=f32):
        return ctx.enter_context(nc.sbuf_tensor(name, shape, dt))

    idx = sb("idx", [P, U, G], u32)
    rbf_t = sb("rbf_t", [2 * R, 2, SETCOLS])
    hid = sb("hid", [P, 2, SETCOLS])
    whole = sb("whole", [C, 2, 2, SETCOLS])
    parts = sb("parts", [P, 2, 2, SETCOLS], f32r)
    xg = sb("xg", [P, U, G, F])
    prod = sb("prod", [P, 2, G, 8, C])
    onehot = sb("onehot", [P, 2, G, W])
    shot = sb("shot", [P, U, G, COMP, W])
    quarters = sb("quarters", [P, 2, F])
    mlp_ps = ctx.enter_context(nc.psum_tensor("mlp_ps", [P, 2, 512], f32))
    radial_ps = ctx.enter_context(nc.psum_tensor("radial_ps", [P, 2, G, F], f32))
    sum_ps = ctx.enter_context(nc.psum_tensor("sum_ps", [P, 2, 512], f32))
    folded_ps = sum_ps[:, :, F:F + 2 * W].rearrange("p b (h w) -> p b h w", h=2)

    rbf_loaded = [sem(f"rbf_loaded{b}") for b in range(2)]
    gathered = [sem(f"gathered{b}") for b in range(U)]
    idx_staged = sem("idx_staged")
    gather_gate = sem("gather_gate")
    x_all_loaded = sem("x_all_loaded")
    mlp_product = sem("mlp_product")
    mlp_active = sem("mlp_active")
    split = sem("split")
    radial_ready = sem("radial_ready")
    onehot_made = sem("onehot_made")
    shot_made = sem("shot_made")
    prod_ready = sem("prod_ready")
    summed = sem("summed")
    moved = sem("moved")
    folded = sem("folded")
    added = sem("added")
    per_pass = [*rbf_loaded, x_all_loaded, idx_staged, gather_gate, mlp_product, mlp_active, split, radial_ready,
                onehot_made, shot_made, prod_ready, summed, moved, folded, added]

    n_passes = nc.values_load(passes[0:1, 0:1], min_val=1, max_val=N // W + 1)
    with nc.Fori(0, n_passes) as k:
        earlier = k * (16 * G * (GROUPS // U))
        with nc.Block() as block:
            @block.sync
            def _(sp):
                def load(i, b):
                    g = i * U + b
                    if not first(g, 4):
                        sp.wait_ge(mlp_product, (g - 2) * 3 + 1)
                    sp.dma_start(rbf_t[:, b % 2, :], rbf[bass.ds(g, 1), :, :].rearrange("a r c -> r (a c)"))\
                      .then_inc(rbf_loaded[b % 2], 16)

                for b in range(2, U):
                    load(0, b)
                cuts = [1 + (GROUPS // U - 1) * k // (COMP + 1) for k in range(COMP + 2)]
                with sp.Fori(cuts[0], cuts[1]) as i:
                    for b in range(U):
                        load(i, b)
                for k in range(COMP):
                    sp.dma_start(x_all[:, k, :], x_sets[:, k, :]).then_inc(x_all_loaded, 16)
                    with sp.Fori(cuts[k + 1], cuts[k + 2]) as i:
                        for b in range(U):
                            load(i, b)
                sp.wait_ge(x_all_loaded, 16 * COMP)

            @block.scalar
            def _(act):
                def stage(i, b):
                    nc.scalar.copy(idx[:, b, :], src_all[:, bass.ds((i * U + b) * G, G)]).then_inc(idx_staged, 1)

                def hidden(i, b, layer):
                    act.wait_ge(mlp_product, (i * U + b) * 3 + layer + 1)
                    if layer < 2:
                        nc.scalar.activation(hid[:, layer, :], mlp_ps[:, b % 2, 0:SETCOLS], ACT.Silu)\
                          .then_inc(mlp_active, 1)
                        return
                    for s in range(2):
                        pre = mlp_ps[s * C:(s + 1) * C, b % 2, 0:SETCOLS]
                        nc.scalar.activation(parts[0:C, b % 2, s, :], pre, ACT.Silu)
                        last = nc.scalar.activation(whole[:, b % 2, s, :], pre, ACT.Silu)
                    last.then_inc(mlp_active, 1)

                def move(i, b):
                    g = i * U + b
                    act.wait_ge(summed, g + 1)
                    if not first(g, 2):
                        act.wait_ge(folded, g - 1)
                    nc.scalar.activation(quarters[:, b % 2, :], sum_ps[:, b % 2, 0:F], ACT.Identity)\
                      .then_inc(moved, 1)

                def step(i, b, to_stage=True, to_hide=True):
                    if to_hide:
                        for layer in range(2):
                            hidden(*following(i, b, 2), layer)
                    if to_stage:
                        act.wait_ge(gathered[b], earlier + (i + 1) * (16 * G))
                        stage(i + 1, b)
                    if to_hide:
                        hidden(*following(i, b, 2), 2)
                    if not first(i * U + b):
                        move(*preceding(i, b))

                for b in range(U):
                    stage(0, b)
                for b in range(2):
                    for layer in range(3):
                        hidden(0, b, layer)
                for b in range(U):
                    step(0, b)
                with act.Fori(1, GROUPS // U - 1) as i:
                    for b in range(U):
                        step(i, b)
                for b in range(U):
                    step(GROUPS // U - 1, b, to_stage=False, to_hide=b < U - 2)
                move(GROUPS // U - 1, U - 1)

            @block.gpsimd
            def _(pool):
                def gather(b):
                    for t in range(G):
                        nc.gpsimd.indirect_dma_start(
                            out=xg[:, b, t, :], out_offset=None, in_=up_table[:, :],
                            in_offset=bass.IndirectOffsetOnAxis(ap=idx[:, b, t:t + 1], axis=0))\
                          .then_inc(gathered[b], 16)

                for b in range(U):
                    pool.wait_ge(idx_staged, b + 1)
                    gather(b)
                with pool.Fori(1, GROUPS // U) as i:
                    for b in range(U):
                        pool.wait_ge(prod_ready, i * U + b - U + 1)
                        pool.wait_ge(idx_staged, i * U + b + 1)
                        pool.sem_inc(gather_gate, 1)
                        gather(b)

            @block.vector
            def _(dve):
                def low_parts(i, b):
                    dve.wait_ge(mlp_active, (i * U + b) * 3 + 3)
                    nc.vector.tensor_tensor(parts[C:P, b % 2], whole[:, b % 2], parts[0:C, b % 2].bitcast(f32),
                                            ALU.subtract).then_inc(split, 1)

                def onehots(i, b):
                    g = i * U + b
                    if not first(g, 2):
                        dve.wait_ge(shot_made, g - 1)
                    nc.vector.tensor_tensor(
                        onehot[:, b % 2, :, :], columns[:, :].unsqueeze(1).broadcast_to([P, G, W]),
                        rel[:, bass.ds(g * G, G)].unsqueeze(2).broadcast_to([P, G, W]), ALU.is_equal)\
                      .then_inc(onehot_made, 1)

                def harmonics(i, b):
                    g = i * U + b
                    dve.wait_ge(onehot_made, g + 1)
                    if not first(g, U):
                        dve.wait_ge(summed, g - U + 1)
                    nc.vector.tensor_tensor(
                        shot[:, b, :, :, :], onehot[:, b % 2, :, :].unsqueeze(2).broadcast_to([P, G, COMP, W]),
                        sh_all[:, bass.ds(g * G, G), :].unsqueeze(3).broadcast_to([P, G, COMP, W]), ALU.mult)\
                      .then_inc(shot_made, 1)

                def products(i, b):
                    g = i * U + b
                    if not first(g, 2):
                        dve.wait_ge(summed, g - 1)
                    dve.wait_ge(radial_ready, i * U + b + 1)
                    dve.wait_ge(gathered[b], earlier + (i + 1) * (16 * G))
                    rad, rows, o = radial_ps[:, b % 2], xg[:, b], prod[:, b % 2]
                    vector_rows = rows[:, :, C:F].rearrange("p t (s c) -> p t s c", c=C)
                    nc.vector.tensor_tensor(
                        o[:, :, 0:5:4, :], rad[:, :, 0:2 * C].rearrange("p t (s c) -> p t s c", c=C),
                        rows[:, :, 0:C].unsqueeze(2).broadcast_to([P, G, 2, C]), ALU.mult)
                    nc.vector.tensor_tensor(
                        o[:, :, 1:4, :], rad[:, :, 2 * C:3 * C].unsqueeze(2).broadcast_to([P, G, 3, C]),
                        vector_rows, ALU.mult)
                    nc.vector.tensor_tensor(
                        o[:, :, 5:8, :], rad[:, :, 3 * C:F].unsqueeze(2).broadcast_to([P, G, 3, C]),
                        vector_rows, ALU.mult).then_inc(prod_ready, 1)

                def add(i, b):
                    g = i * U + b
                    start = dve.value_load(start_row[0:1, bass.ds(g, 1)], min_val=0, max_val=N)
                    dve.wait_ge(folded, g + 1)
                    if not first(g):
                        dve.wait_ge(added, g)
                    window = acc[:, :, bass.ds(start, W)]
                    nc.vector.tensor_tensor(window, folded_ps[:, b % 2], window, ALU.add).then_inc(added, 1)

                def step(i, b, last=False):
                    harmonics(i, b)
                    if first(i * U + b):
                        products(i, b)
                    if not last:
                        low_parts(*following(i, b))
                    if not first(i * U + b):
                        products(i, b)
                    if not last:
                        onehots(*following(i, b))
                    if not first(i * U + b, 2):
                        add(*preceding(i, b, 2))

                dve.wait_ge(sh_loaded, 16)
                low_parts(0, 0)
                onehots(0, 0)
                for b in range(U):
                    step(0, b)
                with dve.Fori(1, GROUPS // U - 1) as i:
                    for b in range(U):
                        step(i, b)
                for b in range(U):
                    step(GROUPS // U - 1, b, last=b == U - 1)
                for b in range(U - 2, U):
                    add(GROUPS // U - 1, b)

            @block.tensor
            def _(pe):
                def layer(i, b, n):
                    g = i * U + b
                    if n == 0:
                        if not first(g, 2):
                            pe.wait_ge(rbf_loaded[b % 2], i * (8 * U) + (b // 2) * 16)
                        if not first(g, 2):
                            pe.wait_ge(mlp_active, (g - 1) * 3)
                    else:
                        pe.wait_ge(mlp_active, g * 3 + n)
                    weight = (m1d[:, :], wts[:, M2D, :], wts[:, M3D, :])[n]
                    data = ((rbf_first if first(g, 2) else rbf_t)[:, b % 2, :], hid[:, 0, :], hid[:, 1, :])[n]
                    nc.tensor.matmul(mlp_ps[:, b % 2, 0:SETCOLS], weight, data, start=True, stop=True)\
                      .then_inc(mlp_product, 1)

                def radial(i, b):
                    g = i * U + b
                    pe.wait_ge(split, g + 1)
                    if not first(g, 2):
                        pe.wait_ge(prod_ready, g - 1)
                    for t in range(G):
                        s, c = divmod(t, G // 2)
                        for n in range(2):
                            last = nc.tensor.matmul(radial_ps[:, b % 2, t, :],
                                                    parts[:, b % 2, s, c * P:(c + 1) * P], m4[n][:, :],
                                                    start=n == 0, stop=n == 1)
                    last.then_inc(radial_ready, 1)

                def segment_sum(i, b, part):
                    g = i * U + b
                    if part == 0:
                        pe.wait_ge(prod_ready, g + 1)
                        if not first(g, 2):
                            pe.wait_ge(added, g - 1)
                    for tile, harmonic, quarter in SCHEDULE[part]:
                        o = sum_ps[quarter * W:(quarter + 1) * W, b % 2, 0:F]
                        terms = prod[:, b % 2, tile]
                        if harmonic == 0:
                            terms = terms[:, 0:4, :]
                        else:
                            o = o.rearrange("n (s c) -> n s c", c=C)[:, 0:harmonic + 1:harmonic, :]
                            terms = terms[:, 4 + harmonic:3:-harmonic, :]
                        last = nc.tensor.matmul(o, shot[:, b, tile, harmonic, :], terms,
                                                start=(tile, harmonic, quarter) in STARTS,
                                                stop=(tile, harmonic, quarter) in STOPS, skip_group_check=True)
                    if part == 1:
                        last.then_inc(summed, 1)

                def folding(i, b):
                    pe.wait_ge(moved, i * U + b + 1)
                    for h in range(2):
                        last = nc.tensor.matmul(folded_ps[:, b % 2, h, :], quarters[:, b % 2, h * P:(h + 1) * P],
                                                fold[:, :], start=True, stop=True)
                    last.then_inc(folded, 1)

                def step(i, b, last=False, to_weigh=True):
                    g = i * U + b
                    for n in range(3):
                        if not last:
                            layer(*following(i, b, 2), n)
                        if n == 0 and to_weigh:
                            radial(i, b)
                        if n == 1 and not first(g, 2):
                            folding(*preceding(i, b, 2))
                        if n and not first(g):
                            segment_sum(*preceding(i, b), n - 1)

                for b in range(2):
                    for n in range(3):
                        layer(0, b, n)
                        if (b, n) == (1, 0):
                            radial(0, 0)
                for b in range(U):
                    step(0, b, to_weigh=b > 0)
                with pe.Fori(1, GROUPS // U - 1) as i:
                    for b in range(U):
                        step(i, b)
                for b in range(U):
                    step(GROUPS // U - 1, b, last=b >= U - 2)
                for part in range(2):
                    segment_sum(GROUPS // U - 1, U - 1, part)
                for b in range(U - 2, U):
                    folding(GROUPS // U - 1, b)

        for s in [*per_pass]:
            nc.gpsimd.sem_clear(s)
        with nc.Block() as block:
            @block.vector
            def _(dve):
                nc.vector.tensor_scalar(rel[:, :], rel[:, :], float(-W), None, ALU.add)
                nc.vector.tensor_scalar(start_row[:, :], start_row[:, :], float(W), float(N), ALU.add, ALU.min)


def node_phase(nc, ctx, x_all, wts, wc0, wc1, gamma0, beta0, gamma1, ident, pair, eps, acc, out, sem):
    def sb(name, shape, dt=f32):
        return ctx.enter_context(nc.sbuf_tensor(name, shape, dt))

    o_all = sb("o_all", [P, COMP, HALF])
    sums = sb("sums", [P, 2, CHUNKS])
    tot = sb("tot", [P, 4])
    stat = sb("stat", [P, 12])
    dense_phase(nc, wts, wc0, wc1, x_all, o_all, sums, acc, sem)
    norm_scales(nc, gamma0, beta0, gamma1, pair, eps, o_all, sums, tot, stat, sem)
    finish(nc, x_all, o_all, stat, ident, eps, out, sem)


def dense_phase(nc, wts, wc0, wc1, x_all, o_all, sums, acc, sem):
    a_ready = sem("a_ready")
    squares = sem("squares")
    lines = sem("lines")
    poly = sem("poly")
    b_ready = sem("b_ready")
    o_ready = sem("o_ready")
    o_moved = sem("o_moved")
    with ExitStack() as ctx:
        def sb(name, shape):
            return ctx.enter_context(nc.sbuf_tensor(name, shape, f32))

        sq = sb("sq", [P, 2, COMP, CH])
        line = sb("line", [P, 2, 2, CH])
        vv = sb("vv", [P, 2, CH])
        q = sb("q", [P, 2, 2, CH])
        basis = sb("basis", [P, 2, COMP, CH])
        junk = sb("junk", [P, 2, 3, CH])
        a_ps = ctx.enter_context(nc.psum_tensor("a_ps", [P, 2, COMP, 256], f32))
        o_ps = ctx.enter_context(nc.psum_tensor("o_ps", [P, 2, COMP, 256], f32))
        block = ctx.enter_context(nc.Block())

        @block.tensor
        def _(pe):
            def linear(i, b):
                j = i * 2 + b
                if not first(j, 2):
                    pe.wait_ge(b_ready, j - 1)
                for k in range(COMP):
                    wide = (LIN0_LO, LIN1_HI, LIN1_LO, LIN1_HI)[k]
                    for s in range(2):
                        node = j * CH + s * HALF
                        last = nc.tensor.matmul(a_ps[s * C:(s + 1) * C, b, k, 0:CH], wts[:, wide, 0:C],
                                                acc[:, k // 2, node:node + CH], start=True, stop=True)
                last.then_inc(a_ready, 1)

            def outputs(i, b):
                j = i * 2 + b
                if not first(j, 2):
                    pe.wait_ge(o_moved, j - 1)
                pe.wait_ge(b_ready, j + 1)
                for k in range(COMP):
                    nc.tensor.matmul(o_ps[:, b, k, 0:CH], wts[:, SC1D if k else SC0D, :],
                                     x_all[:, k, bass.ds(j * CH, CH)], start=True, stop=False)
                    last = nc.tensor.matmul(o_ps[:, b, k, 0:CH], wts[:, WB1D if k else WB0D, :],
                                            basis[:, b, k, :], start=False, stop=True)
                last.then_inc(o_ready, 1)

            for b in range(2):
                linear(0, b)
            for i in range(CHUNKS // 2):
                for b in range(2):
                    if i < CHUNKS // 2 - 1:
                        linear(i + 1, b)
                    outputs(i, b)

        @block.scalar
        def _(act):
            def read(i, b):
                j = i * 2 + b
                act.wait_ge(a_ready, j + 1)
                if not first(j, 2):
                    act.wait_ge(b_ready, j - 1)
                nc.scalar.activation(sq[:, b], a_ps[:, b, :, 0:CH], ACT.Square).then_inc(squares, 1)
                for n, wc in enumerate((wc0, wc1)):
                    last = nc.scalar.activation(line[:, b, n, :], a_ps[:, b, 0, 0:CH], ACT.Identity,
                                                bias=wc[:, 0:1], scale=wc[:, 1:2])
                last.then_inc(lines, 1)

            def move(i, b):
                j = i * 2 + b
                act.wait_ge(o_ready, j + 1)
                nc.scalar.activation(o_all[:, 0, bass.ds(j * CH, CH)], o_ps[:, b, 0, 0:CH], ACT.Identity,
                                     accum_out=sums[:, 0, bass.ds(j, 1)])
                nc.scalar.activation(o_all[:, 1:COMP, bass.ds(j * CH, CH)], o_ps[:, b, 1:COMP, 0:CH], ACT.Identity)
                if not first(j, 2):
                    act.wait_ge(o_moved, j - 1)
                nc.scalar.activation(junk[:, b], o_ps[:, b, 1:COMP, 0:CH], ACT.Square,
                                     accum_out=sums[:, 1, bass.ds(j, 1)]).then_inc(o_moved, 1)

            def step(i):
                for b in range(2):
                    read(i, b)
                    move(i - 1, b)

            for b in range(2):
                read(0, b)
            step(1)
            with act.Fori(2, CHUNKS // 2) as i:
                step(i)
            for b in range(2):
                move(CHUNKS // 2 - 1, b)

        @block.vector
        def _(dve):
            def step(i, b):
                j = i * 2 + b
                dve.wait_ge(squares, j + 1)
                nc.vector.tensor_tensor(vv[:, b], sq[:, b, 1], sq[:, b, 2], ALU.add).then_inc(poly, 1)
                dve.wait_ge(lines, j + 1)
                nc.vector.scalar_tensor_tensor(q[:, b, 0], sq[:, b, 0], wc0[:, 3:4], line[:, b, 0], ALU.mult, ALU.add)
                dve.wait_ge(poly, j * 5 + 1)
                nc.vector.tensor_tensor(vv[:, b], vv[:, b], sq[:, b, 3], ALU.add)
                nc.vector.scalar_tensor_tensor(q[:, b, 1], sq[:, b, 0], wc1[:, 2:3], line[:, b, 1], ALU.mult, ALU.add)\
                  .then_inc(poly, 1)
                dve.wait_ge(poly, j * 5 + 2)
                nc.vector.scalar_tensor_tensor(q[:, b, 0], vv[:, b], wc0[:, 4:5], q[:, b, 0], ALU.mult, ALU.add)\
                  .then_inc(poly, 1)
                nc.vector.scalar_tensor_tensor(q[:, b, 1], vv[:, b], wc1[:, 3:4], q[:, b, 1], ALU.mult, ALU.add)\
                  .then_inc(poly, 1)
                dve.wait_ge(poly, j * 5 + 3)
                nc.vector.tensor_tensor(q[:, b, 0], a_ps[:, b, 0, 0:CH], q[:, b, 0], ALU.mult).then_inc(poly, 1)
                dve.wait_ge(poly, j * 5 + 4)
                if not first(j, 2):
                    dve.wait_ge(o_ready, j - 1)
                nc.vector.tensor_tensor(basis[:, b, 1:COMP, :], a_ps[:, b, 1:COMP, 0:CH],
                                        q[:, b, 1].unsqueeze(1).broadcast_to([P, 3, CH]), ALU.mult)
                dve.wait_ge(poly, j * 5 + 5)
                nc.vector.scalar_tensor_tensor(basis[:, b, 0, :], vv[:, b], wc0[:, 2:3], q[:, b, 0], ALU.mult, ALU.add)\
                  .then_inc(b_ready, 1)

            for b in range(2):
                step(0, b)
            with dve.Fori(1, CHUNKS // 2) as i:
                for b in range(2):
                    step(i, b)


MEAN_NEG, SCALE0, SHIFT0, SCALE1, T0, T1, T2, T3 = range(8)


def norm_scales(nc, gamma0, beta0, gamma1, pair, eps, o_all, sums, tot, stat, sem):
    dve_step = sem("scale_dve")
    pe_step = sem("scale_pe")
    act_step = sem("scale_act")
    with ExitStack() as ctx:
        part = ctx.enter_context(nc.sbuf_tensor("part", [P, 4], f32))
        junk = ctx.enter_context(nc.sbuf_tensor("square_junk", [P, HALF], f32))
        ps = ctx.enter_context(nc.psum_tensor("scale_ps", [P, 512], f32))
        block = ctx.enter_context(nc.Block())

        @block.vector
        def _(dve):
            count = [0]

            def step(ins):
                count[0] += 1
                ins.then_inc(dve_step, 1)
                dve.wait_ge(dve_step, count[0])

            step(nc.vector.tensor_reduce(part[:, 0:1], sums[:, 0, :], X, ALU.add))
            step(nc.vector.tensor_reduce(part[:, 1:2], sums[:, 1, :], X, ALU.add))
            dve.wait_ge(pe_step, 1)
            step(nc.vector.tensor_scalar(stat[:, MEAN_NEG:MEAN_NEG + 1], ps[:, 0:1], -1.0 / N, None, ALU.mult))
            step(nc.vector.tensor_scalar(stat[:, T0:T0 + 1], ps[:, 1:2], 1.0 / (3 * N), EPS, ALU.mult, ALU.add))
            dve.wait_ge(pe_step, 2)
            step(nc.vector.tensor_scalar(stat[:, T1:T1 + 1], ps[:, 2:3], 1.0 / N, EPS, ALU.mult, ALU.add))
            dve.wait_ge(act_step, 3)
            step(nc.vector.reciprocal(stat[:, T2:T2 + 2], tot[:, 0:2]))
            step(nc.vector.tensor_tensor(stat[:, SCALE0:SCALE0 + 1], stat[:, T3:T3 + 1], gamma0[:, :], ALU.mult))
            step(nc.vector.tensor_tensor(stat[:, SCALE1:SCALE1 + 1], stat[:, T2:T2 + 1], gamma1[:, :], ALU.mult))
            step(nc.vector.scalar_tensor_tensor(stat[:, SHIFT0:SHIFT0 + 1], stat[:, MEAN_NEG:MEAN_NEG + 1],
                                                stat[:, SCALE0:SCALE0 + 1], beta0[:, :], ALU.mult, ALU.add))

        @block.tensor
        def _(pe):
            pe.wait_ge(dve_step, 2)
            nc.tensor.matmul(ps[:, 0:2], pair[:, :], part[:, 0:2], start=True, stop=True).then_inc(pe_step, 1)
            pe.wait_ge(act_step, 2)
            pe.wait_ge(dve_step, 4)
            nc.tensor.matmul(ps[:, 2:3], pair[:, :], part[:, 2:3], start=True, stop=True).then_inc(pe_step, 1)

        @block.scalar
        def _(act):
            act.wait_ge(dve_step, 3)
            for lo, n in ((0, HALF), (C, N - HALF)):
                nc.scalar.activation(junk[lo:lo + C, 0:n], o_all[lo:lo + C, 0, 0:n], ACT.Square,
                                     bias=stat[lo:lo + C, MEAN_NEG:MEAN_NEG + 1],
                                     accum_out=part[lo:lo + C, 2:3]).then_inc(act_step, 1)
            act.wait_ge(dve_step, 5)
            nc.scalar.activation(tot[:, 0:2], stat[:, T0:T0 + 2], ACT.Sqrt).then_inc(act_step, 1)


def finish(nc, x_all, o_all, stat, ident, eps, out, sem):
    y0_scaled = sem("y0_scaled")
    y0_made = sem("y0_made")
    y1_made = sem("y1_made")
    y_turned = sem("y_turned")
    ln_stats = sem("ln_stats")
    ln_gate = sem("ln_gate")
    ln_moments = sem("ln_moments")
    ln_root = sem("ln_root")
    ln_inverse = sem("ln_inverse")
    ln_scales = sem("ln_scales")
    res_made = sem("res_made")
    stored = [sem(f"out_stored{b}") for b in range(RING)]
    last_i = NTILES // RING - 1
    with ExitStack() as ctx:
        y = ctx.enter_context(nc.sbuf_tensor("y", [P, RING, COMP, P], f32))
        st = ctx.enter_context(nc.sbuf_tensor("st", [P, RING, 2, 6], f32))
        mv = ctx.enter_context(nc.sbuf_tensor("mv", [P, RING, 2, 2], f32))
        root = ctx.enter_context(nc.sbuf_tensor("root", [P, RING, 2], f32))
        rstd = ctx.enter_context(nc.sbuf_tensor("rstd", [P, RING, 2], f32))
        shift = ctx.enter_context(nc.sbuf_tensor("shift", [P, RING, 2], f32))
        res = ctx.enter_context(nc.sbuf_tensor("res", [P, RING, 2, F], f32))
        y_ps = ctx.enter_context(nc.psum_tensor("y_ps", [P, RING, 2, F], f32))
        block = ctx.enter_context(nc.Block())

        @block.vector
        def _(dve):
            def vectors(i, b):
                g = i * RING + b
                if not first(g, RING):
                    dve.wait_ge(y_turned, g - RING + 1)
                cols = bass.ds(g * P, P)
                nc.vector.scalar_tensor_tensor(y[:, b, 1:COMP, :], o_all[:, 1:COMP, cols],
                                               stat[:, SCALE1:SCALE1 + 1], x_all[:, 1:COMP, cols],
                                               ALU.mult, ALU.add).then_inc(y1_made, 1)

            def statistics(i, b):
                dve.wait_ge(y_turned, i * RING + b + 1)
                for s in range(2):
                    last = nc.vector.bn_stats(st[:, b, s, :], y_ps[:, b, s, :])
                last.then_inc(ln_stats, 1)

            def moments(i, b):
                dve.wait_ge(ln_stats, i * RING + b + 1)
                dve.sem_inc(ln_gate, 1)
                for s in range(2):
                    last = nc.vector.bn_aggr(mv[:, b, s, :], st[:, b, s, :])
                last.then_inc(ln_moments, 1)

            def inverses(i, b):
                dve.wait_ge(ln_root, i * RING + b + 1)
                nc.vector.reciprocal(rstd[:, b, :], root[:, b, :]).then_inc(ln_inverse, 1)

            def shifts(i, b):
                dve.wait_ge(ln_inverse, i * RING + b + 1)
                nc.vector.scalar_tensor_tensor(shift[:, b, :], mv[:, b, :, 0], -1.0, rstd[:, b, :],
                                               ALU.mult, ALU.mult).then_inc(ln_scales, 1)

            def step(i, b, ahead=True):
                statistics(i, b)
                if not first(i * RING + b):
                    inverses(*step_at(i, b, -1, RING))
                if ahead:
                    vectors(*step_at(i, b, 2, RING))
                if not first(i * RING + b):
                    shifts(*step_at(i, b, -1, RING))
                moments(i, b)

            for b in range(2):
                vectors(0, b)
            for b in range(RING):
                step(0, b)
            with dve.Fori(1, last_i) as i:
                for b in range(RING):
                    step(i, b)
            for b in range(RING):
                step(last_i, b, ahead=b + 2 < RING)
            inverses(last_i, RING - 1)
            shifts(last_i, RING - 1)

        @block.gpsimd
        def _(pool):
            def scalars(i, b):
                g = i * RING + b
                pool.wait_ge(y0_scaled, g + 1)
                nc.gpsimd.tensor_tensor(y[:, b, 0, :], y[:, b, 0, :], x_all[:, 0, bass.ds(g * P, P)],
                                        ALU.add).then_inc(y0_made, 1)

            for b in range(RING):
                scalars(0, b)
            with pool.Fori(1, last_i + 1) as i:
                for b in range(RING):
                    scalars(i, b)

        @block.scalar
        def _(act):
            def scale(i, b):
                g = i * RING + b
                if not first(g, RING):
                    act.wait_ge(y_turned, g - RING + 1)
                nc.scalar.activation(y[:, b, 0, :], o_all[:, 0, bass.ds(g * P, P)], ACT.Identity,
                                     scale=stat[:, SCALE0:SCALE0 + 1], bias=stat[:, SHIFT0:SHIFT0 + 1])\
                  .then_inc(y0_scaled, 1)

            def square_root(i, b):
                act.wait_ge(ln_moments, i * RING + b + 1)
                nc.scalar.activation(root[:, b, :], mv[:, b, :, 1], ACT.Sqrt, bias=eps[:, :]).then_inc(ln_root, 1)

            def results(i, b):
                g = i * RING + b
                act.wait_ge(ln_scales, g + 1)
                if not first(g, RING):
                    act.wait_ge(stored[b], i * 32)
                for s in range(2):
                    last = nc.scalar.activation(res[:, b, s, :], y_ps[:, b, s, :], ACT.Identity,
                                                bias=shift[:, b, s:s + 1], scale=rstd[:, b, s:s + 1])
                last.then_inc(res_made, 1)

            def step(i, b, ahead=True):
                if ahead:
                    scale(*step_at(i, b, 3, RING))
                square_root(i, b)
                if not first(i * RING + b):
                    results(*step_at(i, b, -1, RING))

            for b in range(3):
                scale(0, b)
            for b in range(RING):
                step(0, b)
            with act.Fori(1, last_i) as i:
                for b in range(RING):
                    step(i, b)
            for b in range(RING):
                step(last_i, b, ahead=b + 3 < RING)
            results(last_i, RING - 1)

        @block.tensor
        def _(pe):
            def step(i, b):
                g = i * RING + b
                pe.wait_ge(y0_made, g + 1)
                pe.wait_ge(y1_made, g + 1)
                if not first(g, RING):
                    pe.wait_ge(res_made, g - RING + 1)
                vector = y_ps[:, b, :, C:F].rearrange("p s (c k) -> p k s c", k=3)
                for k in range(COMP):
                    last = nc.tensor.transpose(vector[:, k - 1] if k else y_ps[:, b, :, 0:C], y[:, b, k, :],
                                               ident[:, :])
                last.then_inc(y_turned, 1)

            for b in range(RING):
                step(0, b)
            with pe.Fori(1, last_i + 1) as i:
                for b in range(RING):
                    step(i, b)

        @block.sync
        def _(sp):
            def store(i, b, rows=(P, P)):
                g = i * RING + b
                sp.wait_ge(res_made, g + 1)
                for s in range(2):
                    if rows[s]:
                        sp.dma_start(out[bass.ds(g * P + s * HALF, rows[s]), :], res[0:rows[s], b, s, :])\
                          .then_inc(stored[b], 16)

            with sp.Fori(0, last_i) as i:
                for b in range(RING):
                    store(i, b)
            for b in range(RING):
                full = last_i * RING + b - LAST_FULL
                store(last_i, b, (P, P if full < 0 else 0 if full else LAST_ROWS))
            for b in range(RING):
                sp.wait_ge(stored[b], 32 * last_i + (32 if last_i * RING + b <= LAST_FULL else 16))


def kernel(x, src, dst, edge_attr_16, edge_attr_4, **weights):
    import numpy as np
    import concourse.bacc as bacc
    from concourse.bass_utils import run_bass_kernel_spmd

    x, src, dst, edge_attr_16, edge_attr_4 = (np.asarray(a) for a in (x, src, dst, edge_attr_16, edge_attr_4))

    xp = np.zeros((NODES, F), x.dtype)
    xp[:N] = x
    comps = np.concatenate([xp[:, None, :C], xp[:, C:].reshape(NODES, C, 3).transpose(0, 2, 1)], 1)
    x_pairs = np.ascontiguousarray(comps.reshape(NODES, 2, 2 * C).transpose(2, 1, 0))
    x_sets = np.ascontiguousarray(comps.reshape(2, HALF, COMP, C).transpose(0, 3, 2, 1).reshape(P, COMP, HALF))

    def padded(a, fill):
        b = np.full((TILES * P, *a.shape[1:]), fill, a.dtype)
        b[:E] = a
        return b

    arrays = {
        "x_pairs": x_pairs,
        "x_sets": x_sets,
        "src": np.ascontiguousarray(padded(src, 0).reshape(TILES, P).T).view(np.uint32),
        "dst": np.ascontiguousarray(padded(dst, N).reshape(TILES, P).T),
        "sh": np.ascontiguousarray(padded(edge_attr_4, 0).reshape(TILES, P, COMP).transpose(1, 0, 2)),
        "rbf": np.ascontiguousarray(padded(edge_attr_16, 0).reshape(GROUPS, 2, SETCOLS, R)
                                    .transpose(0, 1, 3, 2).reshape(GROUPS, 2 * R, SETCOLS)),
    }
    for name, a in weights.items():
        arrays[name.removeprefix("L0_gnn_")] = np.ascontiguousarray(a)

    nc = bacc.Bacc("TRN2", target_bir_lowering=False, num_devices=1)
    args = {name: nc.dram_tensor(f"in_{name}", a.shape, mybir.dt.from_np(a.dtype), kind="ExternalInput").ap()
            for name, a in arrays.items()}
    out = nc.dram_tensor("out", (N, F), f32, kind="ExternalOutput").ap()
    edge = {name: args.pop(name) for name in ("x_pairs", "x_sets", "src", "dst", "sh", "rbf")}
    build(nc, **edge, w=args, out=out)
    result = run_bass_kernel_spmd(nc, [{f"in_{name}": a for name, a in arrays.items()}], core_ids=[0])
    return result.results[0]["out"]
```
